# Optimizing a Trainium2 kernel written in Bass

```python
import numpy as np
import jax
import jax.numpy as jnp

def _softmax(x, axis=-1):
    return jax.nn.softmax(x, axis=axis)

def _gelu(x):
    return jax.nn.gelu(x, approximate=True)

def _silu(x):
    return jax.nn.silu(x)

def _sigmoid(x):
    return jax.nn.sigmoid(x)

def _layernorm(x, axis=-1, eps=1e-05):
    m = jnp.mean(x, axis=axis, keepdims=True)
    v = jnp.var(x, axis=axis, keepdims=True)
    return (x - m) / jnp.sqrt(v + eps)

def _scatter_add(tgt, idx, src, axis=0):
    return tgt.at[idx].add(src)

def _segment_sum(src, seg, n):
    return jax.ops.segment_sum(src, seg, n)
kernel_name = 'mk_xattn_ffn_d1_seqx_r2_40f416'

def setup_inputs(seed: int=0):
    np.random.seed(seed)
    _w = jnp.asarray

    def _rec_inputs():
        import jax
        import jax.numpy as jnp
        _rk = jax.random.key(seed)
        x = 7.22e-05 + 1 * jax.random.normal(jax.random.fold_in(_rk, 1), (4, 1024, 1024), jnp.float32)
        _lenS = 1024 - jax.random.randint(jax.random.fold_in(_rk, 7), (4,), 0, max(1, 1024 // 4) + 1, jnp.int32)
        _lenS2 = 1024 - jax.random.randint(jax.random.fold_in(_rk, 8), (4,), 0, max(1, 1024 // 4) + 1, jnp.int32)
        _ctx_2048P = jax.random.normal(jax.random.fold_in(_rk, 11), (4, 16, 1024), jnp.float32)
        _ctx_2048c = jax.random.dirichlet(jax.random.fold_in(_rk, 511), 0.3 * jnp.ones((16,), jnp.float32), (4, 1024))
        _ctx_2048t = jnp.einsum('bsk,bkd->bsd', _ctx_2048c, _ctx_2048P)
        _ctx_2048t = _ctx_2048t * jax.lax.rsqrt(jnp.mean(jnp.square(_ctx_2048t)) + 1e-12) * 0.953939
        ctx_2048 = 4.13588e-05 + 0.999923 * (_ctx_2048t + 0.3 * jax.random.normal(jax.random.fold_in(_rk, 611), (4, 1024, 1024), jnp.float32))
        return (x, ctx_2048)
    x, ctx_2048 = _rec_inputs()

    def _L0_xattn_setup():
        import jax, jax.numpy as jnp
        import numpy as np
        N_HEAD = 8
        key = jax.random.key(seed)
        k1, k2, k3 = jax.random.split(key, 3)
        B, D, L = (4, 512, 1024)
        q = jax.random.normal(k1, (B, D, L), dtype=jnp.float32)
        k = jax.random.normal(k2, (B, D, L), dtype=jnp.float32)
        v = jax.random.normal(k3, (B, D, L), dtype=jnp.float32)
        gamma = jnp.ones((), dtype=jnp.float32)
        return {'q': q, 'k': k, 'v': v, 'gamma': gamma}
    _L0_xattn_all = _L0_xattn_setup()
    _L0_xattn_in = {k: v for k, v in _L0_xattn_all.items() if k in ('gamma',)}
    del _L0_xattn_all

    def _L0_ffn_setup():
        import jax, jax.numpy as jnp
        import numpy as np
        B, S, D, K, R = (4, 1024, 1024, 8, 64)
        key = jax.random.key(seed)
        ks = jax.random.split(key, 7)
        x = jax.random.normal(ks[0], (B, S, D), dtype=jnp.float32)
        U = jax.random.normal(ks[1], (K, D, R), dtype=jnp.float32) * 0.02
        V = jax.random.normal(ks[2], (K, R, D), dtype=jnp.float32) * 0.02
        W1 = jax.random.normal(ks[3], (D, D), dtype=jnp.float32) * 0.02
        b1 = jnp.zeros((D,), dtype=jnp.float32)
        W2 = jax.random.normal(ks[4], (D, K), dtype=jnp.float32) * 0.02
        b2 = jnp.zeros((K,), dtype=jnp.float32)
        return {'x': x, 'U': U, 'V': V, 'W1': W1, 'b1': b1, 'W2': W2, 'b2': b2}
    _L0_ffn_all = _L0_ffn_setup()
    _L0_ffn_in = {k: v for k, v in _L0_ffn_all.items() if k in ('U', 'V', 'W1', 'b1', 'W2', 'b2')}
    del _L0_ffn_all
    return {'x': x, 'ctx_2048': ctx_2048, 'L0_xattn_gamma': _L0_xattn_in['gamma'], 'L0_ffn_U': _L0_ffn_in['U'], 'L0_ffn_V': _L0_ffn_in['V'], 'L0_ffn_W1': _L0_ffn_in['W1'], 'L0_ffn_b1': _L0_ffn_in['b1'], 'L0_ffn_W2': _L0_ffn_in['W2'], 'L0_ffn_b2': _L0_ffn_in['b2']}

def reference(x, ctx_2048, L0_xattn_gamma, L0_ffn_U, L0_ffn_V, L0_ffn_W1, L0_ffn_b1, L0_ffn_W2, L0_ffn_b2):
    import jax
    import jax.numpy as jnp

    def _L0_xattn_ref(q, k, v, gamma):
        import jax, jax.numpy as jnp
        import numpy as np
        N_HEAD = 8
        B, Dq, Lq = q.shape
        Dv, Lk = (v.shape[-2], v.shape[-1])
        h = N_HEAD
        dq = Dq // h
        dv = Dv // h
        qh = q.reshape(B, h, dq, Lq)
        kh = k.reshape(B, h, dq, Lk)
        vh = v.reshape(B, h, dv, Lk)
        scale = 1.0 / jnp.sqrt(jnp.asarray(dq, dtype=q.dtype))
        qk = jnp.einsum('bhdq,bhdl->bhql', qh, kh) * scale
        sm = jax.nn.softmax(qk, axis=-1)
        ret = jnp.einsum('bhql,bhdl->bhdq', sm, vh)
        ret = ret.reshape(B, Dv, Lq)
        return gamma * ret

    def _L0_ffn_ref(x, U, V, W1, b1, W2, b2):
        import jax, jax.numpy as jnp
        import numpy as np
        B, S, D, K, R = (4, 1024, 1024, 8, 64)
        h = jax.nn.relu(jnp.einsum('bsd,de->bse', x, W1) + b1)
        alpha = jax.nn.softmax(jnp.einsum('bse,ek->bsk', h, W2) + b2, axis=-1)
        vx = jnp.einsum('krd,bsd->bskr', V, x)
        uvx = jnp.einsum('kdr,bskr->bskd', U, vx)
        out = jnp.einsum('bsk,bskd->bsd', alpha, uvx)
        return out
    x = x + _L0_xattn_ref(_layernorm(x, axis=-1), ctx_2048, ctx_2048, L0_xattn_gamma)
    x = x + _L0_ffn_ref(_layernorm(x, axis=-1), L0_ffn_U, L0_ffn_V, L0_ffn_W1, L0_ffn_b1, L0_ffn_W2, L0_ffn_b2)
    return x

_drawn_inputs = setup_inputs


def setup_inputs(seed=0):
    import zlib

    import numpy as np

    out = dict(_drawn_inputs(seed))
    spreads = {'L0_ffn_b1': (0.0, 2.0), 'L0_ffn_b2': (0.0, 2.0)}
    factors = {'L0_ffn_W1': 7.582, 'L0_ffn_W2': 6.308}
    for name, (base, spread) in spreads.items():
        noise = np.random.default_rng([zlib.crc32(name.encode()), seed]).standard_normal(out[name].shape)
        drawn = base * np.exp(spread * noise) if base else spread * noise
        out[name] = jnp.asarray(drawn.astype(out[name].dtype))
    for name, factor in factors.items():
        out[name] = (out[name] * factor).astype(out[name].dtype)
    return out
```

```python
from contextlib import ExitStack

import concourse.bass as bass
from concourse import mybir

F32 = mybir.dt.float32
F32R = mybir.dt.float32r
ALU = mybir.AluOpType
ACT = mybir.ActivationFunctionType
AX_X = mybir.AxisListType.X

P = 128
BANK = 512
EPS = 1e-5


class SbufMap:

    def __init__(self, nc, offset):
        self.nc, self.at = nc, offset

    def tensor(self, name, shape, dtype=F32):
        size = 4
        for n in shape[1:]:
            size *= n
        got = self.nc.alloc_sbuf_tensor_at(name, shape, dtype, offset=self.at)
        self.at += (size + 31) // 32 * 32
        assert self.at <= self.nc.sbuf_usable_end, name
        return got


def as_f32(tile):
    return tile.bitcast(F32)


def interleave(big, small, lead, rate):
    big, small = list(big), list(small)
    order = big[:lead]
    del big[:lead]
    while big or small:
        order += small[:rate]
        del small[:rate]
        order += big[:1]
        del big[:1]
    return order


def attention(nc, x, ctx, ctx_t, gamma, x1, scratch, preload):
    rows, L = x.shape
    heads = rows // P
    JB = L // P
    HALF = JB // 2
    assert L == 2 * BANK and HALF * P == BANK

    with ExitStack() as stack:
        def psum(name, shape):
            return stack.enter_context(nc.psum_tensor(name, shape, F32))

        def sem(name):
            return stack.enter_context(nc.semaphore(name))

        place = SbufMap(nc, preload["end"])
        pt_hi = [place.tensor(f"pt_hi{b}", [P, JB, BANK], F32R) for b in range(2)]
        pt_lo = [place.tensor(f"pt_lo{b}", [P, JB, BANK], F32R) for b in range(2)]
        q_hi = [place.tensor(f"q_hi{b}", [P, L], F32R) for b in range(2)]
        q_lo = [place.tensor(f"q_lo{b}", [P, L], F32R) for b in range(2)]
        k_hi = [place.tensor(f"k_hi{b}", [P, L], F32R) for b in range(2)]
        k_lo = [place.tensor(f"k_lo{b}", [P, L], F32R) for b in range(2)]
        v_hi = [place.tensor(f"v_hi{b}", [P, JB, P], F32R) for b in range(2)]
        v_lo = [place.tensor(f"v_lo{b}", [P, JB, P], F32R) for b in range(2)]
        x_raw = place.tensor("x_raw", [P, L])
        k_raw = place.tensor("k_raw", [P, L])
        v_raw = place.tensor("v_raw", [P, JB, P])
        x_res = place.tensor("x_res", [P, L])
        q32 = place.tensor("q32", [P, L])
        probs = [place.tensor(f"probs{b}", [P, L]) for b in range(2)]
        gain_row = [place.tensor(f"gain_row{b}", [P, BANK]) for b in range(2)]
        scaled = [place.tensor(f"scaled{b}", [P, BANK]) for b in range(2)]
        x1_out = [place.tensor(f"x1_out{b}", [P, BANK]) for b in range(2)]
        ident = place.tensor("ident", [P, P])
        gamma_col = place.tensor("gamma_col", [P, 1])
        minus_half = place.tensor("minus_half", [P, 1])
        zero_col = place.tensor("zero_col", [P, 1])
        stats = [place.tensor(f"stats{b}", [P, 12]) for b in range(2)]
        mean_var = [place.tensor(f"mean_var{b}", [P, 2]) for b in range(2)]
        var_scaled = [place.tensor(f"var_scaled{b}", [P, 1]) for b in range(2)]
        q_scale = [place.tensor(f"q_scale{b}", [P, 1]) for b in range(2)]
        neg_max = place.tensor("neg_max", [P, JB])
        row_sum = [place.tensor(f"row_sum{b}", [P, JB]) for b in range(2)]
        inv_sum = [place.tensor(f"inv_sum{b}", [P, HALF]) for b in range(2)]
        gain = [place.tensor(f"gain{b}", [P, HALF]) for b in range(2)]

        scores = [psum(f"scores{b}", [P, L]) for b in range(2)]
        turned0 = psum("turned0", [P, 4, P])
        turned1 = [psum(f"turned1{b}", [P, 4, P]) for b in range(2)]
        attended = psum("attended", [P, BANK])

        s_gamma = sem("s_gamma")
        s_x_in, s_k_in, s_v_in, s_res_in = sem("s_x_in"), sem("s_k_in"), sem("s_v_in"), sem("s_res_in")
        s_pre = sem("s_pre")
        s_stat, s_stats, s_var, s_qscale, s_q32 = (sem("s_stat"), sem("s_stats"), sem("s_var"), sem("s_qscale"),
                                                   sem("s_q32"))
        s_qhi, s_qlo, s_ksplit, s_vsplit = sem("s_qhi"), sem("s_qlo"), sem("s_ksplit"), sem("s_vsplit")
        s_scores, s_max, s_exp = sem("s_scores"), sem("s_max"), sem("s_exp")
        s_turn0, s_turn1 = sem("s_turn0"), sem("s_turn1")
        s_hi0, s_hi1, s_lo0, s_lo1 = sem("s_hi0"), sem("s_hi1"), sem("s_lo0"), sem("s_lo1")
        s_pv = sem("s_pv")
        s_inv, s_gain, s_gain_out = sem("s_inv"), sem("s_gain"), sem("s_gain_out")
        s_gain_in, s_scaled, s_added = sem("s_gain_in"), sem("s_scaled"), sem("s_added")
        s_x1 = [sem(f"s_x1{b}") for b in range(2)]
        s_const = sem("s_const")

        block = stack.enter_context(nc.Block())

        def over_heads(eng, slot):
            slot(0, 0, 0, True, False)
            slot(1, JB, 1, False, False)
            with eng.Fori(1, heads // 2 - 1) as pair:
                slot(pair * 2, pair * (2 * JB), 0, False, False)
                slot(pair * 2 + 1, pair * (2 * JB) + JB, 1, False, False)
            slot(heads - 2, (heads - 2) * JB, 0, False, False)
            slot(heads - 1, (heads - 1) * JB, 1, False, True)
            return heads, heads * JB

        @block.sync
        def _(sp):
            def rows_of(h):
                return bass.ts(h, P)

            def load_x(h):
                sp.dma_start(x_raw[:], x[rows_of(h), :]).then_inc(s_x_in, 16)

            def load_k(h):
                sp.dma_start(k_raw[:], ctx[rows_of(h), :]).then_inc(s_k_in, 16)

            def load_v(h):
                sp.dma_start(v_raw[:], ctx_t[rows_of(h), :].rearrange("p (b d) -> p b d", d=P)).then_inc(s_v_in, 16)

            def load_residual(h):
                sp.dma_start(x_res[:], x[rows_of(h), :]).then_inc(s_res_in, 16)

            def spread_gain(half, b):
                sp.wait_ge(s_gain, half + 1)
                sp.dma_start(scratch[bass.ds(half, 1), :].rearrange("a (p j) -> (a p) j", p=P),
                             gain[b][:]).then_inc(s_gain_out, 16)
                sp.wait_ge(s_gain_out, half * 16 + 16)
                sp.dma_start(gain_row[b][:], scratch[bass.ds(half, 1), :].rearrange("a n -> (a n)")
                             .partition_broadcast(P)).then_inc(s_gain_in, 16)

            def store_x1(h, b):
                sp.wait_ge(s_added, h * 2 + b + 1)
                sp.dma_start(x1[rows_of(h), b * BANK:(b + 1) * BANK], x1_out[b][:]).then_inc(s_x1[b], 16)

            def slot(h, n, parity, first, last):
                more = not (isinstance(h, int) and h + 2 >= heads)
                if not first:
                    spread_gain(h * 2 - 1, 1)
                if more:
                    sp.wait_ge(s_ksplit, h * 2 + 4)
                    load_k(h + 2)
                if not first:
                    store_x1(h - 1, 0)
                if more:
                    sp.wait_ge(s_q32, h + 2)
                    load_x(h + 2)
                spread_gain(h * 2, 0)
                if not last:
                    sp.wait_ge(s_vsplit, h * 2 + 2)
                    load_v(h + 1)
                if not first:
                    store_x1(h - 1, 1)
                    load_residual(h)
                if first:
                    for tile, dram in preload["loads"]:
                        sp.dma_start(tile, dram).then_inc(s_pre, 16)

            load_x(0)
            load_k(0)
            sp.dma_start(gamma_col[:], gamma.rearrange("a b -> (a b)").partition_broadcast(P)).then_inc(s_gamma, 16)
            load_v(0)
            load_residual(0)
            sp.wait_ge(s_q32, 1)
            load_x(1)
            sp.wait_ge(s_ksplit, 2)
            load_k(1)
            h, _ = over_heads(sp, slot)
            spread_gain(2 * h - 1, 1)
            store_x1(h - 1, 0)
            store_x1(h - 1, 1)
            for b in range(2):
                sp.wait_ge(s_x1[b], 16 * heads)
            sp.wait_ge(s_pre, 16 * len(preload["loads"]))

        @block.gpsimd
        def _(pool):
            def scale_of_queries(h, b):
                pool.wait_ge(s_var, h + 1)
                nc.gpsimd.tensor_tensor(q_scale[b][:], var_scaled[b][:], minus_half[:], ALU.pow).then_inc(s_qscale, 1)

            def split_keys(h, n, b):
                pool.wait_ge(s_k_in, h * 16 + 16)
                if not (isinstance(h, int) and h < 2):
                    pool.wait_ge(s_scores, n - JB)
                nc.gpsimd.tensor_tensor(k_hi[b][:], k_raw[:], zero_col[:].to_broadcast([P, L]), ALU.add).then_inc(s_ksplit, 1)
                pool.wait_ge(s_ksplit, h * 2 + 1)
                nc.gpsimd.tensor_tensor(k_lo[b][:], k_raw[:], as_f32(k_hi[b][:]), ALU.subtract).then_inc(s_ksplit, 1)

            def split_values(h, n, b):
                pool.wait_ge(s_v_in, h * 16 + 16)
                if not (isinstance(h, int) and h < 2):
                    pool.wait_ge(s_pv, n - JB)
                nc.gpsimd.tensor_tensor(v_hi[b][:], v_raw[:], zero_col[:].unsqueeze(2).to_broadcast([P, JB, P]),
                                        ALU.add).then_inc(s_vsplit, 1)
                pool.wait_ge(s_vsplit, h * 2 + 1)
                nc.gpsimd.tensor_tensor(v_lo[b][:], v_raw[:], as_f32(v_hi[b][:]), ALU.subtract).then_inc(s_vsplit, 1)

            def low_queries(h, b):
                pool.wait_ge(s_qhi, h + 1)
                nc.gpsimd.tensor_tensor(q_lo[b][:], q32[:], as_f32(q_hi[b][:]), ALU.subtract).then_inc(s_qlo, 1)

            def add_residual(h, b):
                pool.wait_ge(s_scaled, h * 2 + b + 1)
                if b == 0:
                    pool.wait_ge(s_res_in, h * 16 + 16)
                if not (isinstance(h, int) and h == 0):
                    pool.wait_ge(s_x1[b], h * 16)
                nc.gpsimd.tensor_tensor(x1_out[b][:], x_res[:, b * BANK:(b + 1) * BANK], scaled[b][:],
                                        ALU.add).then_inc(s_added, 1)

            def slot(h, n, parity, first, last):
                if not last:
                    scale_of_queries(h + 1, 1 - parity)
                    split_keys(h + 1, n + JB, 1 - parity)
                if not first:
                    add_residual(h - 1, 0)
                split_values(h, n, parity)
                if not last:
                    low_queries(h + 1, 1 - parity)
                if not first:
                    add_residual(h - 1, 1)

            nc.gpsimd.memset(minus_half[:], -0.5).then_inc(s_const, 1)
            nc.gpsimd.memset(zero_col[:], 0.0).then_inc(s_const, 1)
            nc.gpsimd.memset(ident[:], 0.0).then_inc(s_const, 1)
            pool.wait_ge(s_const, 3)
            nc.gpsimd.affine_select(out=ident[:], in_=ident[:], compare_op=ALU.not_equal, fill=1.0, base=0,
                                    pattern=[[-1, P]], channel_multiplier=1).then_inc(s_const, 1)
            scale_of_queries(0, 0)
            split_keys(0, 0, 0)
            low_queries(0, 0)
            h, _ = over_heads(pool, slot)
            add_residual(h - 1, 0)
            add_residual(h - 1, 1)

        @block.scalar
        def _(act):
            def high_probs(t, j, n, part, early):
                s_turn, s_hi = (s_turn0, s_hi0) if part == 0 else (s_turn1, s_hi1)
                half = j // HALF
                act.wait_ge(s_turn, t + 1)
                if j % HALF == 0 and not early:
                    act.wait_ge(s_pv, n - JB + 4 * half + (2 if part == 0 else 4))
                src = turned0 if part == 0 else turned1[j % 2]
                col = j % HALF * P
                nc.scalar.activation(pt_hi[half][:, 4 * part:4 * part + 4, col:col + P], src[:],
                                     ACT.Copy).then_inc(s_hi, 1)

            def exps(s, j, b):
                act.wait_ge(s_max, s + 1)
                nc.scalar.activation(probs[j % 2][:], scores[j % 2][:], ACT.Exp, bias=neg_max[:, j:j + 1],
                                     accum_out=row_sum[b][:, j:j + 1]).then_inc(s_exp, 1)

            def high_queries(h, n, b):
                act.wait_ge(s_q32, h + 1)
                if not (isinstance(h, int) and h < 2):
                    act.wait_ge(s_scores, n - JB)
                nc.scalar.activation(q_hi[b][:], q32[:], ACT.Copy).then_inc(s_qhi, 1)

            def slot(h, n, parity, first, last):
                for j in range(JB):
                    back = (n + j - 1, (j - 1) % JB, n if j else n - JB)
                    early = first or (j == 0 and isinstance(h, int) and h == 1)
                    if not (first and j == 0):
                        high_probs(*back, 0, early)
                    exps(n + j, j, parity)
                    if not (first and j == 0):
                        high_probs(*back, 1, early)
                    if j == 4 and not last:
                        high_queries(h + 1, n + JB, 1 - parity)

            high_queries(0, 0, 0)
            h, n = over_heads(act, slot)
            for part in range(2):
                high_probs(n - 1, JB - 1, n - JB, part, False)

        @block.tensor
        def _(pe):
            mm = nc.tensor.matmul

            def score_products(s, j, h, b):
                if j == 0:
                    pe.wait_ge(s_qlo, h + 1)
                    pe.wait_ge(s_ksplit, h * 2 + 2)
                if not (isinstance(s, int) and s < 2):
                    pe.wait_ge(s_exp, s - 1)
                qh, ql = q_hi[b][:, j * P:(j + 1) * P], q_lo[b][:, j * P:(j + 1) * P]
                for q, k, start, stop in ((qh, k_hi, True, False), (qh, k_lo, False, False), (ql, k_hi, False, True)):
                    for c in range(2):
                        last = mm(scores[j % 2][:, c * BANK:(c + 1) * BANK], q, k[b][:, c * BANK:(c + 1) * BANK],
                                  start=start, stop=stop)
                last.then_inc(s_scores, 1)

            def turns(t, j):
                def turn(i):
                    if i == 0:
                        pe.wait_ge(s_exp, t + 1)
                        if not (isinstance(t, int) and t < 1):
                            pe.wait_ge(s_lo0, t)
                    if i == 4 and not (isinstance(t, int) and t < 2):
                        pe.wait_ge(s_lo1, t - 1)
                    dst = turned0 if i < 4 else turned1[j % 2]
                    ins = pe.transpose(dst[:, i % 4, :], probs[j % 2][:, i * P:(i + 1) * P], ident[:])
                    if i == 3:
                        ins.then_inc(s_turn0, 1)
                    if i == 7:
                        ins.then_inc(s_turn1, 1)
                return [lambda i=i: turn(i) for i in range(JB)]

            def attended_products(h, n, half, quarter, b):
                def product(i):
                    if i == 0 and quarter == 0:
                        pe.wait_ge(s_lo0, n + 4 * half + 4)
                        pe.wait_ge(s_lo1, n + 4 * half + 4)
                        if half == 0:
                            pe.wait_ge(s_vsplit, h * 2 + 2)
                        if not (isinstance(h, int) and h == 0 and half == 0):
                            pe.wait_ge(s_scaled, h * 2 + half)
                    lb = 2 * quarter + i // 3
                    v, pt = ((v_hi, pt_hi), (v_hi, pt_lo), (v_lo, pt_hi))[i % 3]
                    ins = mm(attended[:], v[b][:, lb, :], pt[half][:, lb, :],
                             start=(quarter == 0 and i == 0), stop=(quarter == 3 and i == 5))
                    if i == 5:
                        ins.then_inc(s_pv, 1)
                return [lambda i=i: product(i) for i in range(6)]

            def quarter_at(h, n, j, parity, first):
                if j >= 6:
                    return attended_products(h, n, 0, j - 6, parity)
                if first:
                    return []
                if j < 2:
                    return attended_products(h - 1, n - JB, 0, j + 2, 1 - parity)
                return attended_products(h - 1, n - JB, 1, j - 2, 1 - parity)

            def slot(h, n, parity, first, last):
                for j in range(JB):
                    score_products(n + j, j, h, parity)
                    small = [] if first and j == 0 else turns(n + j - 1, (j - 1) % JB)
                    for issue in interleave(quarter_at(h, n, j, parity, first), small, 0, 2):
                        issue()

            pe.wait_ge(s_const, 4)
            h, n = over_heads(pe, slot)
            for j in range(6):
                small = turns(n - 1, JB - 1) if j == 0 else []
                for issue in interleave(quarter_at(h, n, j, 0, False), small, 0, 2):
                    issue()

        @block.vector
        def _(dve):
            def maxima(s, j):
                dve.wait_ge(s_scores, s + 1)
                nc.vector.tensor_reduce(neg_max[:, j:j + 1], scores[j % 2][:], AX_X, ALU.max,
                                        negate=True).then_inc(s_max, 1)

            def low_probs(t, j, part):
                s_hi, s_lo = (s_hi0, s_lo0) if part == 0 else (s_hi1, s_lo1)
                half, col = j // HALF, j % HALF * P
                dve.wait_ge(s_hi, t + 1)
                src = turned0 if part == 0 else turned1[j % 2]
                at = (slice(None), slice(4 * part, 4 * part + 4), slice(col, col + P))
                nc.vector.tensor_tensor(pt_lo[half][at], src[:], as_f32(pt_hi[half][at]),
                                        ALU.subtract).then_inc(s_lo, 1)

            def statistics(h, b):
                dve.wait_ge(s_x_in, h * 16 + 16)
                for c in range(2):
                    nc.vector.bn_stats(stats[b][:, 6 * c:6 * c + 6],
                                       x_raw[:, c * BANK:(c + 1) * BANK]).then_inc(s_stat, 1)

            def variance(h, b):
                nc.vector.bn_aggr(mean_var[b][:], stats[b][:]).then_inc(s_stats, 1)
                dve.wait_ge(s_stats, h + 1)
                nc.vector.tensor_scalar(var_scaled[b][:], mean_var[b][:, 1:2], EPS, float(P),
                                        ALU.add, ALU.mult).then_inc(s_var, 1)

            def queries(h, b):
                dve.wait_ge(s_qscale, h + 1)
                if not (isinstance(h, int) and h == 0):
                    dve.wait_ge(s_qlo, h)
                nc.vector.tensor_scalar(q32[:], x_raw[:], mean_var[b][:, 0:1], q_scale[b][:],
                                        ALU.subtract, ALU.mult).then_inc(s_q32, 1)

            def gains(h, half, b):
                number = h * 2 + half
                nc.vector.reciprocal(inv_sum[half][:], row_sum[b][:, half * HALF:(half + 1) * HALF]).then_inc(s_inv, 1)
                if not (isinstance(h, int) and h == 0):
                    dve.wait_ge(s_gain_out, number * 16 - 16)
                else:
                    dve.wait_ge(s_gamma, 16)
                dve.wait_ge(s_inv, number + 1)
                nc.vector.tensor_scalar(gain[half][:], inv_sum[half][:], gamma_col[:], None,
                                        ALU.mult).then_inc(s_gain, 1)

            def scale_attended(h, n, half):
                dve.wait_ge(s_pv, n + 4 * half + 4)
                dve.wait_ge(s_gain_in, h * 32 + (half * 16 + 16))
                if not (isinstance(h, int) and h == 0):
                    dve.wait_ge(s_added, h * 2 + half - 1)
                nc.vector.tensor_tensor(scaled[half][:].rearrange("p (j a) -> p j a", j=HALF),
                                        attended[:].rearrange("p (j a) -> p j a", j=HALF),
                                        gain_row[half][:].rearrange("p (a j) -> p j a", j=HALF),
                                        ALU.mult).then_inc(s_scaled, 1)

            def slot(h, n, parity, first, last):
                for j in range(JB):
                    s = n + j
                    if j in (2, 6) and not first:
                        scale_attended(h - 1, n - JB, j // 4)
                    maxima(s, j)
                    if j == 1 and not last:
                        dve.wait_ge(s_stat, h * 2 + 4)
                    if not (first and j < 1):
                        low_probs(s - 1, (j - 1) % JB, 0)
                    if not (first and j < 2):
                        low_probs(s - 2, (j - 2) % JB, 1)
                    if j == 0 and not last:
                        statistics(h + 1, 1 - parity)
                    if j == 1 and not last:
                        variance(h + 1, 1 - parity)
                    if j == 1 and not first:
                        gains(h - 1, 1, 1 - parity)
                    if j == 3 and not last:
                        queries(h + 1, 1 - parity)
                    if j == 5:
                        gains(h, 0, parity)

            statistics(0, 0)
            dve.wait_ge(s_stat, 2)
            variance(0, 0)
            queries(0, 0)
            h, n = over_heads(dve, slot)
            low_probs(n - 1, JB - 1, 0)
            low_probs(n - 2, JB - 2, 1)
            low_probs(n - 1, JB - 1, 1)
            gains(h - 1, 1, 1)
            scale_attended(h - 1, n - JB, 0)
            scale_attended(h - 1, n - JB, 1)


def mixture(nc, x1, b1, w2, b2, weights, out):
    rows, D = x1.shape
    tiles = rows // P
    KB = D // P
    E = w2.shape[1]
    KR = weights["v_hi"].shape[2]
    RB = KR // P
    assert D == 2 * BANK and KR == BANK
    w1_raw, w1_hi, w1_lo = weights["w1_raw"], weights["w1_hi"], weights["w1_lo"]
    v_raw, v_hi, v_lo = weights["v_raw"], weights["v_hi"], weights["v_lo"]
    u_raw, u_hi, u_lo = weights["u_raw"], weights["u_hi"], weights["u_lo"]

    with ExitStack() as stack:
        def psum(name, shape):
            return stack.enter_context(nc.psum_tensor(name, shape, F32))

        def sem(name):
            return stack.enter_context(nc.semaphore(name))

        place = SbufMap(nc, weights["end"])
        x_in = [place.tensor(f"x_in{b}", [P, D]) for b in range(2)]
        x_keep = [place.tensor(f"x_keep{b}", [P, D]) for b in range(2)]
        normed = place.tensor("normed", [P, D])
        nt_hi = [place.tensor(f"nt_hi{b}", [P, KB, P], F32R) for b in range(2)]
        nt_lo = [place.tensor(f"nt_lo{b}", [P, KB, P], F32R) for b in range(2)]
        hidden = place.tensor("hidden", [P, D])
        ht_hi = place.tensor("ht_hi", [P, KB, P], F32R)
        ht_lo = place.tensor("ht_lo", [P, KB, P], F32R)
        gated = place.tensor("gated", [P, KR])
        gt_hi = place.tensor("gt_hi", [P, RB, P], F32R)
        gt_lo = place.tensor("gt_lo", [P, RB, P], F32R)
        b1_row = place.tensor("b1_row", [P, D])
        b2_row = place.tensor("b2_row", [P, E])
        w2_raw = place.tensor("w2_raw", [P, KB, E])
        w2_both = place.tensor("w2_both", [P, KB, 2 * E], F32R)
        out_half = [place.tensor(f"out_half{b}", [P, BANK]) for b in range(2)]
        ident = place.tensor("ident2", [P, P])
        minus_half = place.tensor("minus_half2", [P, 1])
        zero_col = place.tensor("zero_col2", [P, 1])
        stats = place.tensor("stats2", [P, 12])
        mean_var = place.tensor("mean_var2", [P, 2])
        var_eps = place.tensor("var_eps", [P, 1])
        rstd = place.tensor("rstd", [P, 1])
        logit_part = place.tensor("logit_part", [P, E])
        logits = place.tensor("logits", [P, E])
        neg_max = place.tensor("neg_max2", [P, 1])
        e_logits = place.tensor("e_logits", [P, E])
        e_sum = place.tensor("e_sum", [P, 1])
        inv_sum = place.tensor("inv_sum2", [P, 1])

        turned = [psum(f"turned_m{b}", [P, 4, P]) for b in range(2)]
        h_ps = psum("h_ps", [P, D])
        vx_ps = psum("vx_ps", [P, KR])
        l_ps = psum("l_ps", [P, BANK])
        y_ps = [psum(f"y_ps{b}", [P, BANK]) for b in range(2)]

        s_small, s_u_in, s_const = sem("s_small"), sem("s_u_in"), sem("s_const2")
        s_w2, s_whi, s_wlo = sem("s_w2"), sem("s_whi"), sem("s_wlo")
        s_xin = [sem(f"s_xin{b}") for b in range(2)]
        s_stat, s_stats, s_var, s_rstd, s_normed, s_kept = (sem("s_stat2"), sem("s_stats2"), sem("s_var2"),
                                                            sem("s_rstd"), sem("s_normed"), sem("s_kept"))
        s_tn, s_nhi, s_nlo = ([sem(f"{n}{b}") for b in range(2)] for n in ("s_tn", "s_nhi", "s_nlo"))
        s_th, s_hhi, s_hlo = ([sem(f"{n}{b}") for b in range(2)] for n in ("s_th", "s_hhi", "s_hlo"))
        s_tg, s_ghi, s_glo = sem("s_tg"), sem("s_ghi"), sem("s_glo")
        s_w1, s_hidden, s_v, s_l = sem("s_w1"), sem("s_hidden"), sem("s_v"), sem("s_l")
        s_lpart, s_logits, s_negmax, s_elog, s_inv, s_gate = (sem("s_lpart"), sem("s_logits"), sem("s_negmax"),
                                                              sem("s_elog"), sem("s_inv2"), sem("s_gate"))
        s_y, s_yadd = [sem(f"s_y{b}") for b in range(2)], [sem(f"s_yadd{b}") for b in range(2)]
        s_out = [sem(f"s_out{b}") for b in range(2)]

        block = stack.enter_context(nc.Block())

        def over_tiles(eng, slot):
            slot(0, 0, 0, True, False)
            slot(1, 0, 1, False, False)
            with eng.Fori(1, tiles // 2 - 1) as pair:
                slot(pair * 2, pair, 0, False, False)
                slot(pair * 2 + 1, pair, 1, False, False)
            slot(tiles - 2, tiles // 2 - 1, 0, False, False)
            slot(tiles - 1, tiles // 2 - 1, 1, False, True)

        chunks = [(w1_raw[:, k, :], w1_hi[:, k, :], w1_lo[:, k, :]) for k in range(KB)]
        chunks += [(v_raw[:, k:k + 2, :], v_hi[:, k:k + 2, :], v_lo[:, k:k + 2, :]) for k in range(0, KB, 2)]
        v_ready = len(chunks)
        chunks += [(u_raw[:, k, :], u_hi[:, k, :], u_lo[:, k, :]) for k in range(RB)]

        @block.sync
        def _(sp):
            def load(t, b):
                sp.dma_start(x_in[b][:], x1[bass.ts(t, P), :]).then_inc(s_xin[b], 16)

            def store(t, b):
                sp.wait_ge(s_yadd[b], t + 1)
                sp.dma_start(out[bass.ts(t, P), b * BANK:(b + 1) * BANK], out_half[b][:]).then_inc(s_out[b], 16)

            def slot(t, pair, parity, first, last):
                if not last and not (isinstance(t, int) and t + 2 >= tiles):
                    sp.wait_ge(s_kept, t + 1)
                    sp.wait_ge(s_normed, t + 1)
                    load(t + 2, parity)
                if not first:
                    store(t - 1, 0)
                    store(t - 1, 1)

            load(0, 0)
            sp.dma_start(w2_raw[:], w2.rearrange("(k p) e -> p k e", p=P)).then_inc(s_small, 16)
            sp.dma_start(b1_row[:], b1.partition_broadcast(P)).then_inc(s_small, 16)
            sp.dma_start(b2_row[:], b2.partition_broadcast(P)).then_inc(s_small, 16)
            load(1, 1)
            sp.dma_start(u_raw[:], weights["u_dram"]).then_inc(s_u_in, 16)
            over_tiles(sp, slot)
            for b in range(2):
                store(tiles - 1, b)
                sp.wait_ge(s_out[b], 16 * tiles)

        @block.gpsimd
        def _(pool):
            def factor(t):
                pool.wait_ge(s_var, t + 1)
                nc.gpsimd.tensor_tensor(rstd[:], var_eps[:], minus_half[:], ALU.pow).then_inc(s_rstd, 1)

            def keep(t, pair, b, free):
                if free is not None:
                    pool.wait_ge(s_yadd[1], free)
                pool.wait_ge(s_xin[b], pair * 16 + 16)
                nc.gpsimd.tensor_tensor(x_keep[b][:], x_in[b][:], zero_col[:].to_broadcast([P, D]), ALU.add).then_inc(s_kept, 1)

            def slot(t, pair, parity, first, last):
                if not last:
                    factor(t + 1)
                    keep(t + 1, pair + parity, 1 - parity, None if first else t)

            nc.gpsimd.memset(minus_half[:], -0.5).then_inc(s_const, 1)
            nc.gpsimd.memset(zero_col[:], 0.0).then_inc(s_const, 1)
            nc.gpsimd.memset(ident[:], 0.0).then_inc(s_const, 1)
            pool.wait_ge(s_const, 3)
            nc.gpsimd.affine_select(out=ident[:], in_=ident[:], compare_op=ALU.not_equal, fill=1.0, base=0,
                                    pattern=[[-1, P]], channel_multiplier=1).then_inc(s_const, 1)
            factor(0)
            keep(0, 0, 0, None)
            over_tiles(pool, slot)

        @block.scalar
        def _(act):
            def high(dst, src, s_in, s_done, count, func=ACT.Copy):
                act.wait_ge(s_in, count)
                nc.scalar.activation(dst, src, func).then_inc(s_done, 1)

            def high_normed(t, b):
                for c in range(2):
                    high(nt_hi[b][:, 4 * c:4 * c + 4, :], turned[c][:], s_tn[c], s_nhi[c], t + 1)

            def slot(t, pair, parity, first, last):
                if not first:
                    high(gt_hi[:], turned[0][:], s_tg, s_ghi, t)
                if not last:
                    high_normed(t + 1, 1 - parity)
                for c in range(2):
                    high(ht_hi[:, 4 * c:4 * c + 4, :], turned[c][:], s_th[c], s_hhi[c], t + 1, ACT.Relu)
                act.wait_ge(s_negmax, t + 1)
                nc.scalar.activation(e_logits[:], logits[:], ACT.Exp, bias=neg_max[:],
                                     accum_out=e_sum[:]).then_inc(s_elog, 1)

            act.wait_ge(s_small, 48)
            nc.scalar.activation(w2_both[:, :, 0:E], w2_raw[:], ACT.Copy).then_inc(s_w2, 1)
            high_normed(0, 0)
            for n, (raw, hi, lo) in enumerate(chunks):
                if n == v_ready:
                    act.wait_ge(s_u_in, 16)
                nc.scalar.activation(hi, raw, ACT.Copy).then_inc(s_whi, 1)
            over_tiles(act, slot)
            high(gt_hi[:], turned[0][:], s_tg, s_ghi, tiles)

        @block.tensor
        def _(pe):
            mm = nc.tensor.matmul

            def hidden_products(t, b, k0, k1):
                def product(k, c, i):
                    if i == 0 and c == 0:
                        if k % 4 == 0:
                            pe.wait_ge(s_nlo[k // 4], t + 1)
                        if isinstance(t, int) and t == 0:
                            pe.wait_ge(s_wlo, k + 1)
                        elif k == 0:
                            pe.wait_ge(s_hidden, t * 2)
                    n, w = ((nt_hi, w1_hi), (nt_hi, w1_lo), (nt_lo, w1_hi))[i]
                    ins = mm(h_ps[:, c * BANK:(c + 1) * BANK], n[b][:, k, :], w[:, k, c * BANK:(c + 1) * BANK],
                             start=(k == 0 and i == 0), stop=(k == KB - 1 and i == 2))
                    if k == KB - 1 and i == 2:
                        ins.then_inc(s_w1, 1)
                return [lambda k=k, c=c, i=i: product(k, c, i) for k in range(k0, k1) for c in range(2)
                        for i in range(3)]

            def value_products(t, b):
                def product(k, i):
                    if k == 0 and i == 0:
                        if isinstance(t, int) and t == 0:
                            pe.wait_ge(s_wlo, v_ready)
                        else:
                            pe.wait_ge(s_gate, t)
                    n, w = ((nt_hi, v_hi), (nt_hi, v_lo), (nt_lo, v_hi))[i]
                    ins = mm(vx_ps[:], n[b][:, k, :], w[:, k, :], start=(k == 0 and i == 0),
                             stop=(k == KB - 1 and i == 2))
                    if k == KB - 1 and i == 2:
                        ins.then_inc(s_v, 1)
                return [lambda k=k, i=i: product(k, i) for k in range(KB) for i in range(3)]

            def expert_products(t, c):
                def product(r, i):
                    if r == 0 and i == 0:
                        if c == 0:
                            pe.wait_ge(s_glo, t + 1)
                            if isinstance(t, int) and t == 0:
                                pe.wait_ge(s_wlo, len(chunks))
                        if not (isinstance(t, int) and t == 0):
                            pe.wait_ge(s_yadd[c], t)
                    g, w = ((gt_hi, u_hi), (gt_hi, u_lo), (gt_lo, u_hi))[i]
                    ins = mm(y_ps[c][:], g[:, r, :], w[:, r, c * BANK:(c + 1) * BANK], start=(r == 0 and i == 0),
                             stop=(r == RB - 1 and i == 2))
                    if r == RB - 1 and i == 2:
                        ins.then_inc(s_y[c], 1)
                return [lambda r=r, i=i: product(r, i) for r in range(RB) for i in range(3)]

            def router_products(t):
                def product(k, i):
                    if i == 0 and k % 4 == 0:
                        pe.wait_ge(s_hlo[k // 4], t + 1)
                        if k == 0 and isinstance(t, int) and t == 0:
                            pe.wait_ge(s_w2, 2)
                        elif k == 0:
                            pe.wait_ge(s_logits, t)
                    if i == 0:
                        mm(l_ps[:, 0:2 * E], ht_hi[:, k, :], w2_both[:, k, :], start=(k == 0), stop=(k == KB - 1),
                           skip_group_check=True)
                    else:
                        ins = mm(l_ps[:, 0:E], ht_lo[:, k, :], w2_both[:, k, 0:E], start=False, stop=(k == KB - 1),
                                 skip_group_check=True)
                        if k == KB - 1:
                            ins.then_inc(s_l, 1)
                return [lambda k=k, i=i: product(k, i) for k in range(KB) for i in range(2)]

            def turn_normed(t):
                def turn(i):
                    if i == 0:
                        pe.wait_ge(s_normed, t + 1)
                    if i % 4 == 0 and not (isinstance(t, int) and t == 0):
                        if i == 0 and not (isinstance(t, int) and t == 1):
                            pe.wait_ge(s_glo, t - 1)
                        elif i == 4 and not (isinstance(t, int) and t == 1):
                            pe.wait_ge(s_hlo[1], t - 1)
                        elif isinstance(t, int) and t == 1:
                            pe.wait_ge(s_nlo[i // 4], t)
                    ins = pe.transpose(turned[i // 4][:, i % 4, :], normed[:, i * P:(i + 1) * P], ident[:])
                    if i % 4 == 3:
                        ins.then_inc(s_tn[i // 4], 1)
                return [lambda i=i: turn(i) for i in range(KB)]

            def turn_hidden(t, last):
                def turn(i):
                    if i % 4 == 0:
                        pe.wait_ge(s_hidden, t * 2 + i // 4 + 1)
                        if not last:
                            pe.wait_ge(s_nlo[i // 4], t + 2)
                        elif i == 0:
                            pe.wait_ge(s_glo, t)
                    ins = pe.transpose(turned[i // 4][:, i % 4, :], hidden[:, i * P:(i + 1) * P], ident[:])
                    if i % 4 == 3:
                        ins.then_inc(s_th[i // 4], 1)
                return [lambda i=i: turn(i) for i in range(KB)]

            def turn_gated(t):
                def turn(i):
                    if i == 0:
                        pe.wait_ge(s_gate, t + 1)
                        pe.wait_ge(s_hlo[0], t + 1)
                    ins = pe.transpose(turned[0][:, i, :], gated[:, i * P:(i + 1) * P], ident[:])
                    if i == RB - 1:
                        ins.then_inc(s_tg, 1)
                return [lambda i=i: turn(i) for i in range(RB)]

            def issue_all(functions):
                for issue in functions:
                    issue()

            def slot(t, pair, parity, first, last):
                issue_all(hidden_products(t, parity, 0, 3))
                issue_all(interleave(hidden_products(t, parity, 3, KB), [] if first else turn_gated(t - 1), 0, 2))
                values = value_products(t, parity)
                issue_all(interleave(values[:12], [] if last else turn_normed(t + 1), 0, 2))
                issue_all(interleave(values[12:], turn_hidden(t, last), 4, 2))
                if not first:
                    issue_all(expert_products(t - 1, 0))
                issue_all(interleave([] if first else expert_products(t - 1, 1), router_products(t), 0, 2))

            pe.wait_ge(s_const, 4)
            issue_all(turn_normed(0))
            over_tiles(pe, slot)
            issue_all(turn_gated(tiles - 1))
            issue_all(expert_products(tiles - 1, 0))
            issue_all(expert_products(tiles - 1, 1))

        @block.vector
        def _(dve):
            def statistics(t, pair, b):
                dve.wait_ge(s_xin[b], pair * 16 + 16)
                for c in range(2):
                    nc.vector.bn_stats(stats[:, 6 * c:6 * c + 6],
                                       x_in[b][:, c * BANK:(c + 1) * BANK]).then_inc(s_stat, 1)

            def normalise(t, b):
                nc.vector.bn_aggr(mean_var[:], stats[:]).then_inc(s_stats, 1)
                dve.wait_ge(s_stats, t + 1)
                nc.vector.tensor_scalar(var_eps[:], mean_var[:, 1:2], EPS, None, ALU.add).then_inc(s_var, 1)
                dve.wait_ge(s_rstd, t + 1)
                if not (isinstance(t, int) and t == 0):
                    dve.wait_ge(s_tn[1], t)
                nc.vector.tensor_scalar(normed[:], x_in[b][:], mean_var[:, 0:1], rstd[:],
                                        ALU.subtract, ALU.mult).then_inc(s_normed, 1)

            def low_normed(t, b):
                for c in range(2):
                    dve.wait_ge(s_nhi[c], t + 1)
                    nc.vector.tensor_tensor(nt_lo[b][:, 4 * c:4 * c + 4, :], turned[c][:],
                                            as_f32(nt_hi[b][:, 4 * c:4 * c + 4, :]), ALU.subtract).then_inc(s_nlo[c], 1)

            def add_b1(t):
                for c in range(2):
                    dve.wait_ge(s_w1, t * 2 + c + 1)
                    if c == 0 and not (isinstance(t, int) and t == 0):
                        dve.wait_ge(s_th[1], t)
                    nc.vector.tensor_tensor(hidden[:, c * BANK:(c + 1) * BANK], h_ps[:, c * BANK:(c + 1) * BANK],
                                            b1_row[:, c * BANK:(c + 1) * BANK], ALU.add).then_inc(s_hidden, 1)

            def low_hidden(t):
                for c in range(2):
                    dve.wait_ge(s_hhi[c], t + 1)
                    nc.vector.scalar_tensor_tensor(ht_lo[:, 4 * c:4 * c + 4, :], turned[c][:], 0.0,
                                                   as_f32(ht_hi[:, 4 * c:4 * c + 4, :]), ALU.max,
                                                   ALU.subtract).then_inc(s_hlo[c], 1)

            def low_gated(t):
                dve.wait_ge(s_ghi, t + 1)
                nc.vector.tensor_tensor(gt_lo[:], turned[0][:], as_f32(gt_hi[:]), ALU.subtract).then_inc(s_glo, 1)

            def add_residual(t, b, c):
                dve.wait_ge(s_y[c], t + 1)
                if c == 0:
                    dve.wait_ge(s_kept, t + 1)
                if not (isinstance(t, int) and t == 0):
                    dve.wait_ge(s_out[c], t * 16)
                nc.vector.tensor_tensor(out_half[c][:], y_ps[c][:], x_keep[b][:, c * BANK:(c + 1) * BANK],
                                        ALU.add).then_inc(s_yadd[c], 1)

            def gate(t):
                dve.wait_ge(s_l, t + 1)
                nc.vector.tensor_tensor(logit_part[:], l_ps[:, 0:E], b2_row[:], ALU.add).then_inc(s_lpart, 1)
                dve.wait_ge(s_lpart, t + 1)
                nc.vector.tensor_tensor(logits[:], l_ps[:, E:2 * E], logit_part[:], ALU.add).then_inc(s_logits, 1)
                dve.wait_ge(s_logits, t + 1)
                nc.vector.tensor_reduce(neg_max[:], logits[:], AX_X, ALU.max, negate=True).then_inc(s_negmax, 1)
                dve.wait_ge(s_elog, t + 1)
                nc.vector.reciprocal(inv_sum[:], e_sum[:]).then_inc(s_inv, 1)
                dve.wait_ge(s_inv, t + 1)
                dve.wait_ge(s_v, t + 1)
                nc.vector.scalar_tensor_tensor(gated[:].rearrange("p (e r) -> p e r", e=E),
                                               vx_ps[:].rearrange("p (e r) -> p e r", e=E), inv_sum[:],
                                               e_logits[:].unsqueeze(2).to_broadcast([P, E, KR // E]),
                                               ALU.mult, ALU.mult).then_inc(s_gate, 1)

            def slot(t, pair, parity, first, last):
                if not last:
                    statistics(t + 1, pair + parity, 1 - parity)
                    dve.wait_ge(s_stat, t * 2 + 4)
                if not first:
                    low_gated(t - 1)
                if not last:
                    normalise(t + 1, 1 - parity)
                add_b1(t)
                if not last:
                    low_normed(t + 1, 1 - parity)
                low_hidden(t)
                if not first:
                    add_residual(t - 1, 1 - parity, 0)
                gate(t)
                if not first:
                    add_residual(t - 1, 1 - parity, 1)

            dve.wait_ge(s_w2, 1)
            nc.vector.tensor_tensor(w2_both[:, :, E:2 * E], w2_raw[:], as_f32(w2_both[:, :, 0:E]),
                                    ALU.subtract).then_inc(s_w2, 1)
            statistics(0, 0, 0)
            dve.wait_ge(s_stat, 2)
            normalise(0, 0)
            low_normed(0, 0)
            for n, (raw, hi, lo) in enumerate(chunks):
                dve.wait_ge(s_whi, n + 1)
                nc.vector.tensor_tensor(lo, raw, as_f32(hi), ALU.subtract).then_inc(s_wlo, 1)
            over_tiles(dve, slot)
            low_gated(tiles - 1)
            add_residual(tiles - 1, 1, 0)
            add_residual(tiles - 1, 1, 1)


def cross_attention_and_mixture(nc, x, ctx, ctx_t, gamma, u_t, v_t, w1, b1, w2, b2, out):
    D, KR = v_t.shape
    x1 = nc.dram_tensor("x1", tuple(x.shape), F32, kind="Internal").ap()
    scratch = nc.dram_tensor("gains", (2 * x.shape[0] // P, BANK), F32, kind="Internal").ap()

    base = (nc.sbuf_base + 31) // 32 * 32
    raw, low = SbufMap(nc, base), SbufMap(nc, base)
    weights = {}
    for name, blocks, width in (("w1", D // P, D), ("v", D // P, KR)):
        weights[name + "_raw"] = raw.tensor(name + "_raw", [P, blocks, width])
        weights[name + "_lo"] = low.tensor(name + "_lo", [P, blocks, width], F32R)
    preload = {
        "end": raw.at,
        "loads": [(weights["w1_raw"][:], w1.rearrange("(k p) e -> p k e", p=P)),
                  (weights["v_raw"][:], v_t.rearrange("(k p) r -> p k r", p=P))],
    }
    attention(nc, x, ctx, ctx_t, gamma, x1, scratch, preload)

    weights["u_raw"] = raw.tensor("u_raw", [P, KR // P, D])
    weights["u_lo"] = low.tensor("u_lo", [P, KR // P, D], F32R)
    weights["w1_hi"] = raw.tensor("w1_hi", [P, D // P, D], F32R)
    weights["v_hi"] = raw.tensor("v_hi", [P, D // P, KR], F32R)
    weights["u_hi"] = raw.tensor("u_hi", [P, KR // P, D], F32R)
    weights["u_dram"] = u_t.rearrange("(k p) d -> p k d", p=P)
    weights["end"] = raw.at
    mixture(nc, x1, b1, w2, b2, weights, out)


def kernel(**inputs):
    import numpy as np
    import concourse.bacc as bacc
    from concourse.bass_utils import run_bass_kernel_spmd

    x = np.asarray(inputs["x"])
    ctx = np.asarray(inputs["ctx_2048"])
    B, S, D = x.shape
    heads = B * S // P
    U, V = np.asarray(inputs["L0_ffn_U"]), np.asarray(inputs["L0_ffn_V"])
    experts, _, rank = U.shape
    ctx_t = ctx.reshape(heads, P, D // P, P).transpose(0, 3, 2, 1)
    arrays = {
        "x": x.reshape(B * S, D),
        "ctx": ctx.reshape(B * S, D),
        "ctx_t": ctx_t.reshape(B * S, D),
        "gamma": np.asarray(inputs["L0_xattn_gamma"]).reshape(1, 1),
        "u_t": U.transpose(0, 2, 1).reshape(experts * rank, D),
        "v_t": V.reshape(experts * rank, D).transpose(1, 0),
        "w1": np.asarray(inputs["L0_ffn_W1"]),
        "b1": np.asarray(inputs["L0_ffn_b1"]),
        "w2": np.asarray(inputs["L0_ffn_W2"]),
        "b2": np.asarray(inputs["L0_ffn_b2"]),
    }
    arrays = {"in_" + name: np.ascontiguousarray(a) for name, a in arrays.items()}
    nc = bacc.Bacc("TRN2", target_bir_lowering=False, num_devices=1)
    args = [nc.dram_tensor(name, a.shape, mybir.dt.from_np(a.dtype), kind="ExternalInput").ap()
            for name, a in arrays.items()]
    args.append(nc.dram_tensor("out", (B * S, D), F32, kind="ExternalOutput").ap())
    cross_attention_and_mixture(nc, *args)
    result = run_bass_kernel_spmd(nc, [arrays], core_ids=[0])
    return result.results[0]["out"].reshape(B, S, D)
```

```python
from contextlib import ExitStack

import concourse.bass as bass
from concourse import mybir

F32 = mybir.dt.float32
F32R = mybir.dt.float32r
ALU = mybir.AluOpType
ACT = mybir.ActivationFunctionType
AX_X = mybir.AxisListType.X

P = 128
BANK = 512
FIRST = 4
EPS = 1e-5


class SbufMap:

    def __init__(self, nc, offset):
        self.nc, self.at = nc, offset

    def tensor(self, name, shape, dtype=F32):
        size = 4
        for n in shape[1:]:
            size *= n
        got = self.nc.alloc_sbuf_tensor_at(name, shape, dtype, offset=self.at)
        self.at += (size + 31) // 32 * 32
        assert self.at <= self.nc.sbuf_usable_end, name
        return got


def as_f32(tile):
    return tile.bitcast(F32)


def interleave(big, small, lead, rate):
    big, small = list(big), list(small)
    order = big[:lead]
    del big[:lead]
    while big or small:
        order += small[:rate]
        del small[:rate]
        order += big[:1]
        del big[:1]
    return order


def attention(nc, x, ctx, ctx_t, gamma, x1, scratch, shared):
    rows, L = x.shape
    heads = rows // P
    JB = L // P
    HALF = JB // 2
    assert L == 2 * BANK and HALF * P == BANK

    with ExitStack() as stack:
        def psum(name, shape):
            return stack.enter_context(nc.psum_tensor(name, shape, F32))

        def sem(name):
            return stack.enter_context(nc.semaphore(name))

        place = SbufMap(nc, shared["loaded_end"])
        pt_hi = [place.tensor(f"pt_hi{b}", [P, JB, BANK], F32R) for b in range(2)]
        pt_lo = [place.tensor(f"pt_lo{b}", [P, JB, BANK], F32R) for b in range(2)]
        assert place.at == shared["first_at"]
        q_hi, q_lo, k_hi, k_lo = ([place.tensor(f"{name}0", [P, L], F32R)] for name in ("q_hi", "q_lo", "k_hi", "k_lo"))
        for name, tiles in (("q_hi", q_hi), ("q_lo", q_lo), ("k_hi", k_hi), ("k_lo", k_lo)):
            tiles.append(place.tensor(f"{name}1", [P, L], F32R))
        v_hi = [place.tensor(f"v_hi{b}", [P, JB, P], F32R) for b in range(2)]
        v_lo = [place.tensor(f"v_lo{b}", [P, JB, P], F32R) for b in range(2)]
        x_raw = place.tensor("x_raw", [P, L])
        k_raw = place.tensor("k_raw", [P, L])
        v_raw = place.tensor("v_raw", [P, JB, P])
        x_res = place.tensor("x_res", [P, L])
        q32 = place.tensor("q32", [P, L])
        probs = [place.tensor(f"probs{b}", [P, L]) for b in range(2)]
        gain_row = [place.tensor(f"gain_row{b}", [P, BANK]) for b in range(2)]
        scaled = [place.tensor(f"scaled{b}", [P, BANK]) for b in range(2)]
        top = SbufMap(nc, shared["top_at"])
        x1_out = [top.tensor(f"x1_out{b}", [P, BANK]) for b in range(2)]
        ident = place.tensor("ident", [P, P])
        first_mean_var = [place.tensor(f"first_mean_var{k}", [P, 2]) for k in range(FIRST)]
        first_var_eps = [place.tensor(f"first_var_eps{k}", [P, 1]) for k in range(FIRST)]
        first_rstd = [place.tensor(f"first_rstd{k}", [P, 1]) for k in range(FIRST)]
        gamma_col = place.tensor("gamma_col", [P, 1])
        minus_half = place.tensor("minus_half", [P, 1])
        zero_col = place.tensor("zero_col", [P, 1])
        stats = [place.tensor(f"stats{b}", [P, 12]) for b in range(2)]
        mean_var = [place.tensor(f"mean_var{b}", [P, 2]) for b in range(2)]
        var_scaled = [place.tensor(f"var_scaled{b}", [P, 1]) for b in range(2)]
        q_scale = [place.tensor(f"q_scale{b}", [P, 1]) for b in range(2)]
        neg_max = place.tensor("neg_max", [P, JB])
        row_sum = [place.tensor(f"row_sum{b}", [P, JB]) for b in range(2)]
        inv_sum = [place.tensor(f"inv_sum{b}", [P, HALF]) for b in range(2)]
        gain = [place.tensor(f"gain{b}", [P, HALF]) for b in range(2)]

        assert place.at <= shared["top_at"]

        scores = [psum(f"scores{b}", [P, L]) for b in range(2)]
        turned0 = psum("turned0", [P, 4, P])
        turned1 = [psum(f"turned1{b}", [P, 4, P]) for b in range(2)]
        attended = psum("attended", [P, BANK])

        s_gamma = sem("s_gamma")
        s_x_in, s_k_in, s_v_in, s_res_in = sem("s_x_in"), sem("s_k_in"), sem("s_v_in"), sem("s_res_in")
        s_pre = sem("s_pre")
        s_stat, s_stats, s_var, s_qscale, s_q32 = (sem("s_stat"), sem("s_stats"), sem("s_var"), sem("s_qscale"),
                                                   sem("s_q32"))
        s_qhi, s_qlo, s_ksplit, s_vsplit = sem("s_qhi"), sem("s_qlo"), sem("s_ksplit"), sem("s_vsplit")
        s_scores, s_max, s_exp = sem("s_scores"), sem("s_max"), sem("s_exp")
        s_turn0, s_turn1 = sem("s_turn0"), sem("s_turn1")
        s_hi0, s_hi1, s_lo0, s_lo1 = sem("s_hi0"), sem("s_hi1"), sem("s_lo0"), sem("s_lo1")
        s_pv = sem("s_pv")
        s_inv, s_gain, s_gain_out = sem("s_inv"), sem("s_gain"), sem("s_gain_out")
        s_gain_in, s_scaled, s_added = sem("s_gain_in"), sem("s_scaled"), sem("s_added")
        s_x1 = shared["s_x1"]
        s_const = sem("s_const")
        s_f_in = [sem(f"s_f_in{k}") for k in range(FIRST)]
        s_f_stat, s_f_stats, s_f_var, s_f_rstd, s_f_n = (sem("s_f_stat"), sem("s_f_stats"), sem("s_f_var"),
                                                         sem("s_f_rstd"), sem("s_f_n"))
        first_n = shared["first_n"]

        block = stack.enter_context(nc.Block())

        def over_heads(eng, slot):
            slot(0, 0, 0, True, False)
            slot(1, JB, 1, False, False)
            with eng.Fori(1, heads // 2 - 1) as pair:
                slot(pair * 2, pair * (2 * JB), 0, False, False)
                slot(pair * 2 + 1, pair * (2 * JB) + JB, 1, False, False)
            slot(heads - 2, (heads - 2) * JB, 0, False, False)
            slot(heads - 1, (heads - 1) * JB, 1, False, True)
            return heads, heads * JB

        @block.sync
        def _(sp):
            def rows_of(h):
                return bass.ts(h, P)

            def load_x(h):
                sp.dma_start(x_raw[:], x[rows_of(h), :]).then_inc(s_x_in, 16)

            def load_k(h):
                sp.dma_start(k_raw[:], ctx[rows_of(h), :]).then_inc(s_k_in, 16)

            def load_v(h):
                sp.dma_start(v_raw[:], ctx_t[rows_of(h), :].rearrange("p (b d) -> p b d", d=P)).then_inc(s_v_in, 16)

            def load_residual(h):
                sp.dma_start(x_res[:], x[rows_of(h), :]).then_inc(s_res_in, 16)

            def spread_gain(half, b):
                sp.wait_ge(s_gain, half + 1)
                sp.dma_start(scratch[bass.ds(half, 1), :].rearrange("a (p j) -> (a p) j", p=P),
                             gain[b][:]).then_inc(s_gain_out, 16)
                sp.wait_ge(s_gain_out, half * 16 + 16)
                sp.dma_start(gain_row[b][:], scratch[bass.ds(half, 1), :].rearrange("a n -> (a n)")
                             .partition_broadcast(P)).then_inc(s_gain_in, 16)

            def store_x1(h, b):
                sp.wait_ge(s_added, h * 2 + b + 1)
                sp.dma_start(x1[rows_of(h), b * BANK:(b + 1) * BANK], x1_out[b][:]).then_inc(s_x1[b], 16)

            def load_first(n):
                sp.wait_ge(s_scores, n)
                for b in range(2):
                    sp.wait_ge(s_x1[b], 16 * len(first_n))
                for k, tile in enumerate(first_n):
                    sp.dma_start(tile[:], x1[bass.ts(k, P), :]).then_inc(s_f_in[k], 16)

            def preload_weights(count):
                for tile, dram in loads[:count]:
                    sp.dma_start(tile, dram).then_inc(s_pre, 16)
                del loads[:count]

            loads = list(shared["loads"])

            def slot(h, n, parity, first, last):
                early = isinstance(h, int) and h < 2
                more = not (isinstance(h, int) and h + 2 >= heads)
                if last:
                    load_first(n)
                if not first:
                    spread_gain(h * 2 - 1, 1)
                if not last:
                    sp.wait_ge(s_vsplit, h * 2 + 2)
                    load_v(h + 1)
                if not first:
                    store_x1(h - 1, 0)
                if early and not first:
                    preload_weights(4)
                if more:
                    sp.wait_ge(s_ksplit, h * 2 + 4)
                    load_k(h + 2)
                    sp.wait_ge(s_q32, h + 2)
                    load_x(h + 2)
                spread_gain(h * 2, 0)
                if not first:
                    store_x1(h - 1, 1)
                    load_residual(h)
                if early:
                    preload_weights(6 if first else 5)

            load_x(0)
            load_k(0)
            sp.dma_start(gamma_col[:], gamma.rearrange("a b -> (a b)").partition_broadcast(P)).then_inc(s_gamma, 16)
            load_v(0)
            load_residual(0)
            sp.wait_ge(s_q32, 1)
            load_x(1)
            sp.wait_ge(s_ksplit, 2)
            load_k(1)
            h, _ = over_heads(sp, slot)
            spread_gain(2 * h - 1, 1)
            store_x1(h - 1, 0)
            store_x1(h - 1, 1)
            sp.wait_ge(s_pre, 16 * len(shared["loads"]))

        @block.gpsimd
        def _(pool):
            def scale_of_queries(h, b):
                pool.wait_ge(s_var, h + 1)
                nc.gpsimd.tensor_tensor(q_scale[b][:], var_scaled[b][:], minus_half[:], ALU.pow).then_inc(s_qscale, 1)

            def split_keys(h, n, b):
                pool.wait_ge(s_k_in, h * 16 + 16)
                if not (isinstance(h, int) and h < 2):
                    pool.wait_ge(s_scores, n - JB)
                nc.gpsimd.tensor_tensor(k_hi[b][:], k_raw[:], zero_col[:].to_broadcast([P, L]), ALU.add).then_inc(s_ksplit, 1)
                pool.wait_ge(s_ksplit, h * 2 + 1)
                nc.gpsimd.tensor_tensor(k_lo[b][:], k_raw[:], as_f32(k_hi[b][:]), ALU.subtract).then_inc(s_ksplit, 1)

            def split_values(h, n, b):
                pool.wait_ge(s_v_in, h * 16 + 16)
                if not (isinstance(h, int) and h < 2):
                    pool.wait_ge(s_pv, n - JB)
                nc.gpsimd.tensor_tensor(v_hi[b][:], v_raw[:], zero_col[:].unsqueeze(2).to_broadcast([P, JB, P]),
                                        ALU.add).then_inc(s_vsplit, 1)
                pool.wait_ge(s_vsplit, h * 2 + 1)
                nc.gpsimd.tensor_tensor(v_lo[b][:], v_raw[:], as_f32(v_hi[b][:]), ALU.subtract).then_inc(s_vsplit, 1)

            def low_queries(h, b):
                pool.wait_ge(s_qhi, h + 1)
                nc.gpsimd.tensor_tensor(q_lo[b][:], q32[:], as_f32(q_hi[b][:]), ALU.subtract).then_inc(s_qlo, 1)

            def add_residual(h, b):
                pool.wait_ge(s_scaled, h * 2 + b + 1)
                if b == 0:
                    pool.wait_ge(s_res_in, h * 16 + 16)
                if not (isinstance(h, int) and h == 0):
                    pool.wait_ge(s_x1[b], h * 16)
                nc.gpsimd.tensor_tensor(x1_out[b][:], x_res[:, b * BANK:(b + 1) * BANK], scaled[b][:],
                                        ALU.add).then_inc(s_added, 1)

            def normalise_first(k):
                pool.wait_ge(s_f_var, k + 1)
                nc.gpsimd.tensor_tensor(first_rstd[k][:], first_var_eps[k][:], minus_half[:], ALU.pow).then_inc(s_f_rstd, 1)
                pool.wait_ge(s_f_rstd, k + 1)
                nc.gpsimd.tensor_scalar(first_n[k][:], first_n[k][:], first_mean_var[k][:, 0:1], first_rstd[k][:],
                                        ALU.subtract, ALU.mult).then_inc(s_f_n, 1)

            def slot(h, n, parity, first, last):
                split_values(h, n, parity)
                if not first:
                    add_residual(h - 1, 0)
                if last:
                    normalise_first(0)
                    normalise_first(1)
                if not last:
                    scale_of_queries(h + 1, 1 - parity)
                    split_keys(h + 1, n + JB, 1 - parity)
                    low_queries(h + 1, 1 - parity)
                if not first:
                    add_residual(h - 1, 1)

            nc.gpsimd.memset(minus_half[:], -0.5).then_inc(s_const, 1)
            nc.gpsimd.memset(zero_col[:], 0.0).then_inc(s_const, 1)
            nc.gpsimd.memset(ident[:], 0.0).then_inc(s_const, 1)
            pool.wait_ge(s_const, 3)
            nc.gpsimd.affine_select(out=ident[:], in_=ident[:], compare_op=ALU.not_equal, fill=1.0, base=0,
                                    pattern=[[-1, P]], channel_multiplier=1).then_inc(s_const, 1)
            scale_of_queries(0, 0)
            h, _ = over_heads(pool, slot)
            normalise_first(2)
            normalise_first(3)
            add_residual(h - 1, 0)
            add_residual(h - 1, 1)

        @block.scalar
        def _(act):
            def high_probs(t, j, n, part, early):
                s_turn, s_hi = (s_turn0, s_hi0) if part == 0 else (s_turn1, s_hi1)
                half = j // HALF
                act.wait_ge(s_turn, t + 1)
                if j % HALF == 0 and not early:
                    act.wait_ge(s_pv, n - JB + 4 * half + (2 if part == 0 else 4))
                src = turned0 if part == 0 else turned1[j % 2]
                col = j % HALF * P
                nc.scalar.activation(pt_hi[half][:, 4 * part:4 * part + 4, col:col + P], src[:],
                                     ACT.Copy).then_inc(s_hi, 1)

            def exps(s, j, b):
                act.wait_ge(s_max, s + 1)
                nc.scalar.activation(probs[j % 2][:], scores[j % 2][:], ACT.Exp, bias=neg_max[:, j:j + 1],
                                     accum_out=row_sum[b][:, j:j + 1]).then_inc(s_exp, 1)

            def high_queries(h, n, b):
                act.wait_ge(s_q32, h + 1)
                if not (isinstance(h, int) and h < 2):
                    act.wait_ge(s_scores, n - JB)
                nc.scalar.activation(q_hi[b][:], q32[:], ACT.Copy).then_inc(s_qhi, 1)

            def slot(h, n, parity, first, last):
                for j in range(JB):
                    back = (n + j - 1, (j - 1) % JB, n if j else n - JB)
                    early = first or (j == 0 and isinstance(h, int) and h == 1)
                    if not (first and j == 0):
                        high_probs(*back, 0, early)
                    exps(n + j, j, parity)
                    if not (first and j == 0):
                        high_probs(*back, 1, early)
                    if j == 5 and not last:
                        high_queries(h + 1, n + JB, 1 - parity)

            act.wait_ge(s_k_in, 16)
            nc.scalar.activation(k_hi[0][:], k_raw[:], ACT.Copy).then_inc(s_ksplit, 1)
            high_queries(0, 0, 0)
            h, n = over_heads(act, slot)
            for part in range(2):
                high_probs(n - 1, JB - 1, n - JB, part, False)

        @block.tensor
        def _(pe):
            mm = nc.tensor.matmul

            def score_products(s, j, h, b):
                if j == 0:
                    pe.wait_ge(s_qlo, h + 1)
                    pe.wait_ge(s_ksplit, h * 2 + 2)
                if not (isinstance(s, int) and s < 2):
                    pe.wait_ge(s_exp, s - 1)
                qh, ql = q_hi[b][:, j * P:(j + 1) * P], q_lo[b][:, j * P:(j + 1) * P]
                for q, k, start, stop in ((qh, k_hi, True, False), (qh, k_lo, False, False), (ql, k_hi, False, True)):
                    for c in range(2):
                        last = mm(scores[j % 2][:, c * BANK:(c + 1) * BANK], q, k[b][:, c * BANK:(c + 1) * BANK],
                                  start=start, stop=stop)
                last.then_inc(s_scores, 1)

            def turns(t, j):
                def turn(i):
                    if i == 0:
                        pe.wait_ge(s_exp, t + 1)
                        if not (isinstance(t, int) and t < 1):
                            pe.wait_ge(s_lo0, t)
                    if i == 4 and not (isinstance(t, int) and t < 2):
                        pe.wait_ge(s_lo1, t - 1)
                    dst = turned0 if i < 4 else turned1[j % 2]
                    ins = pe.transpose(dst[:, i % 4, :], probs[j % 2][:, i * P:(i + 1) * P], ident[:])
                    if i == 3:
                        ins.then_inc(s_turn0, 1)
                    if i == 7:
                        ins.then_inc(s_turn1, 1)
                return [lambda i=i: turn(i) for i in range(JB)]

            def attended_products(h, n, half, quarter, b):
                def product(i):
                    if i == 0 and quarter == 0:
                        pe.wait_ge(s_lo0, n + 4 * half + 4)
                        pe.wait_ge(s_lo1, n + 4 * half + 4)
                        if half == 0:
                            pe.wait_ge(s_vsplit, h * 2 + 2)
                        if not (isinstance(h, int) and h == 0 and half == 0):
                            pe.wait_ge(s_scaled, h * 2 + half)
                    lb = 2 * quarter + i // 3
                    v, pt = ((v_hi, pt_hi), (v_hi, pt_lo), (v_lo, pt_hi))[i % 3]
                    ins = mm(attended[:], v[b][:, lb, :], pt[half][:, lb, :],
                             start=(quarter == 0 and i == 0), stop=(quarter == 3 and i == 5))
                    if i == 5:
                        ins.then_inc(s_pv, 1)
                return [lambda i=i: product(i) for i in range(6)]

            def quarter_at(h, n, j, parity, first):
                if j >= 6:
                    return attended_products(h, n, 0, j - 6, parity)
                if first:
                    return []
                if j < 2:
                    return attended_products(h - 1, n - JB, 0, j + 2, 1 - parity)
                return attended_products(h - 1, n - JB, 1, j - 2, 1 - parity)

            def slot(h, n, parity, first, last):
                for j in range(JB):
                    score_products(n + j, j, h, parity)
                    small = [] if first and j == 0 else turns(n + j - 1, (j - 1) % JB)
                    for issue in interleave(quarter_at(h, n, j, parity, first), small, 0, 2):
                        issue()

            pe.wait_ge(s_const, 4)
            h, n = over_heads(pe, slot)
            for j in range(6):
                small = turns(n - 1, JB - 1) if j == 0 else []
                for issue in interleave(quarter_at(h, n, j, 0, False), small, 0, 2):
                    issue()

        @block.vector
        def _(dve):
            def maxima(s, j):
                dve.wait_ge(s_scores, s + 1)
                nc.vector.tensor_reduce(neg_max[:, j:j + 1], scores[j % 2][:], AX_X, ALU.max,
                                        negate=True).then_inc(s_max, 1)

            def low_probs(t, j, part):
                s_hi, s_lo = (s_hi0, s_lo0) if part == 0 else (s_hi1, s_lo1)
                half, col = j // HALF, j % HALF * P
                dve.wait_ge(s_hi, t + 1)
                src = turned0 if part == 0 else turned1[j % 2]
                at = (slice(None), slice(4 * part, 4 * part + 4), slice(col, col + P))
                nc.vector.tensor_tensor(pt_lo[half][at], src[:], as_f32(pt_hi[half][at]),
                                        ALU.subtract).then_inc(s_lo, 1)

            def statistics(h, b, c):
                if c == 0:
                    dve.wait_ge(s_x_in, h * 16 + 16)
                nc.vector.bn_stats(stats[b][:, 6 * c:6 * c + 6],
                                   x_raw[:, c * BANK:(c + 1) * BANK]).then_inc(s_stat, 1)

            def variance(h, b):
                nc.vector.bn_aggr(mean_var[b][:], stats[b][:]).then_inc(s_stats, 1)
                dve.wait_ge(s_stats, h + 1)
                nc.vector.tensor_scalar(var_scaled[b][:], mean_var[b][:, 1:2], EPS, float(P),
                                        ALU.add, ALU.mult).then_inc(s_var, 1)

            def queries(h, b):
                dve.wait_ge(s_qscale, h + 1)
                if not (isinstance(h, int) and h == 0):
                    dve.wait_ge(s_qlo, h)
                nc.vector.tensor_scalar(q32[:], x_raw[:], mean_var[b][:, 0:1], q_scale[b][:],
                                        ALU.subtract, ALU.mult).then_inc(s_q32, 1)

            def gains(h, half, b):
                number = h * 2 + half
                nc.vector.reciprocal(inv_sum[half][:], row_sum[b][:, half * HALF:(half + 1) * HALF]).then_inc(s_inv, 1)
                if not (isinstance(h, int) and h == 0):
                    dve.wait_ge(s_gain_out, number * 16 - 16)
                else:
                    dve.wait_ge(s_gamma, 16)
                dve.wait_ge(s_inv, number + 1)
                nc.vector.tensor_scalar(gain[half][:], inv_sum[half][:], gamma_col[:], None,
                                        ALU.mult).then_inc(s_gain, 1)

            def scale_attended(h, n, half):
                dve.wait_ge(s_pv, n + 4 * half + 4)
                dve.wait_ge(s_gain_in, h * 32 + (half * 16 + 16))
                if not (isinstance(h, int) and h == 0):
                    dve.wait_ge(s_added, h * 2 + half - 1)
                nc.vector.tensor_tensor(scaled[half][:].rearrange("p (j a) -> p j a", j=HALF),
                                        attended[:].rearrange("p (j a) -> p j a", j=HALF),
                                        gain_row[half][:].rearrange("p (a j) -> p j a", j=HALF),
                                        ALU.mult).then_inc(s_scaled, 1)

            def first_statistics(part):
                k, c = part // 2, part % 2
                dve.wait_ge(s_f_in[k], 16)
                nc.vector.bn_stats(stats[k % 2][:, 6 * c:6 * c + 6],
                                   first_n[k][:, c * BANK:(c + 1) * BANK]).then_inc(s_f_stat, 1)

            def first_variance(k):
                dve.wait_ge(s_f_stat, 2 * k + 2)
                nc.vector.bn_aggr(first_mean_var[k][:], stats[k % 2][:]).then_inc(s_f_stats, 1)
                dve.wait_ge(s_f_stats, k + 1)
                nc.vector.tensor_scalar(first_var_eps[k][:], first_mean_var[k][:, 1:2], EPS, None,
                                        ALU.add).then_inc(s_f_var, 1)

            def slot(h, n, parity, first, last):
                for j in range(JB):
                    s = n + j
                    maxima(s, j)
                    if j == 3 and not last:
                        dve.wait_ge(s_stat, h * 2 + 4)
                    if not (first and j < 1):
                        low_probs(s - 1, (j - 1) % JB, 0)
                    if not (first and j < 2):
                        low_probs(s - 2, (j - 2) % JB, 1)
                    if j in (1, 5) and not first:
                        scale_attended(h - 1, n - JB, j // 4)
                    if last and j > 0:
                        first_statistics(j - 1)
                        if j % 2 == 0:
                            first_variance(j // 2 - 1)
                    if j in (0, 2) and not last:
                        statistics(h + 1, 1 - parity, j // 2)
                    if j == 3 and not last:
                        variance(h + 1, 1 - parity)
                    if j == 2 and not first:
                        gains(h - 1, 1, 1 - parity)
                    if j == 4 and not last:
                        queries(h + 1, 1 - parity)
                    if j == 6:
                        gains(h, 0, parity)

            statistics(0, 0, 0)
            statistics(0, 0, 1)
            dve.wait_ge(s_stat, 2)
            variance(0, 0)
            queries(0, 0)
            dve.wait_ge(s_ksplit, 1)
            nc.vector.tensor_tensor(k_lo[0][:], k_raw[:], as_f32(k_hi[0][:]), ALU.subtract).then_inc(s_ksplit, 1)
            dve.wait_ge(s_qhi, 1)
            nc.vector.tensor_tensor(q_lo[0][:], q32[:], as_f32(q_hi[0][:]), ALU.subtract).then_inc(s_qlo, 1)
            h, n = over_heads(dve, slot)
            first_statistics(JB - 1)
            first_variance(3)
            low_probs(n - 1, JB - 1, 0)
            low_probs(n - 2, JB - 2, 1)
            low_probs(n - 1, JB - 1, 1)
            gains(h - 1, 1, 1)
            scale_attended(h - 1, n - JB, 0)
            scale_attended(h - 1, n - JB, 1)


def mixture(nc, x1, shared, out):
    rows, D = x1.shape
    tiles = rows // P
    GT = BANK // P
    groups = tiles // GT
    KB = D // P
    E = shared["w2_raw"].shape[2]
    KR = shared["v_hi"].shape[2]
    RB = KR // P
    assert D == 2 * BANK and KR == BANK and RB == 4 and GT == FIRST and KB == 2 * GT
    w1_raw, w1_hi, w1_lo = shared["w1_raw"], shared["w1_hi"], shared["w1_lo"]
    v_raw, v_hi, v_lo = shared["v_raw"], shared["v_hi"], shared["v_lo"]
    u_raw, u_hi, u_lo = shared["u_raw"], shared["u_hi"], shared["u_lo"]
    w2_raw, b1_col, b2_row = shared["w2_raw"], shared["b1_col"], shared["b2_row"]

    with ExitStack() as stack:
        def psum(name, shape):
            return stack.enter_context(nc.psum_tensor(name, shape, F32))

        def sem(name):
            return stack.enter_context(nc.semaphore(name))

        place = SbufMap(nc, shared["end"])
        first_n, x_in, normed = shared["first_n"], shared["first_n"][:2], shared["first_n"][2:]
        nt_hi = place.tensor("nt_hi", [P, KB, BANK], F32R)
        nt_lo = place.tensor("nt_lo", [P, KB, BANK], F32R)
        ht_hi = [place.tensor(f"ht_hi{b}", [P, BANK], F32R) for b in range(2)]
        low, after = SbufMap(nc, place.at), SbufMap(nc, place.at)
        hidden = [place.tensor(f"hidden{b}", [P, BANK]) for b in range(2)]
        ht_lo = [low.tensor(f"ht_lo{b}", [P, BANK], F32R) for b in range(2)]
        logits_t = after.tensor("logits_t", [2 * E, BANK])
        gated = [place.tensor(f"gated{b}", [P, KR]) for b in range(2)]
        gt_hi = [place.tensor(f"gt_hi{b}", [P, RB, P], F32R) for b in range(2)]
        gt_lo = [place.tensor(f"gt_lo{b}", [P, RB, P], F32R) for b in range(2)]
        top = SbufMap(nc, shared["top_at"])
        result = [top.tensor(f"result{b}", [P, BANK]) for b in range(4)]
        w2_both = place.tensor("w2_both", [P, KB, 2 * E], F32R)
        ident = place.tensor("ident2", [P, P])
        minus_half = place.tensor("minus_half2", [P, 1])
        stats = place.tensor("stats2", [P, 12])
        mean_var = [place.tensor(f"mean_var2{k}", [P, 2]) for k in range(GT)]
        var_eps = [place.tensor(f"var_eps{k}", [P, 1]) for k in range(GT)]
        rstd = [place.tensor(f"rstd{k}", [P, 1]) for k in range(GT)]
        logit_part = place.tensor("logit_part", [P, GT, E])
        logits = place.tensor("logits", [P, GT, E])
        centred = place.tensor("centred", [P, GT, E])
        neg_max = place.tensor("neg_max2", [P, GT])
        e_logits = place.tensor("e_logits", [P, GT, E])
        e_sum = place.tensor("e_sum", [P, GT])
        inv_sum = place.tensor("inv_sum2", [P, GT])
        alpha = place.tensor("alpha", [P, GT, E])

        assert place.at <= shared["top_at"]

        turned = [psum(f"turned_m{b}", [P, 4, P]) for b in range(2)]
        work = [psum(f"work{b}", [P, BANK]) for b in range(2)]
        lt_ps = psum("lt_ps", [P, BANK])
        l_ps = psum("l_ps", [P, GT, P])
        y_ps = [psum(f"y_ps{b}", [P, BANK]) for b in range(2)]

        s_u_in, s_const = sem("s_u_in"), sem("s_const2")
        s_w2, s_whi, s_wlo = sem("s_w2"), sem("s_whi"), sem("s_wlo")
        s_xin = [sem(f"s_xin{b}") for b in range(2)]
        s_stat, s_stats, s_var, s_rstd, s_normed = (sem("s_stat2"), sem("s_stats2"), sem("s_var2"),
                                                    sem("s_rstd"), sem("s_normed"))
        s_turn, s_hi, s_lo = sem("s_turn"), sem("s_hi"), sem("s_lo")
        s_hidden, s_hhi, s_relu, s_hlo = sem("s_hidden"), sem("s_hhi"), sem("s_relu"), sem("s_hlo")
        s_route, s_lt_out, s_l = sem("s_route"), sem("s_lt_out"), sem("s_l")
        s_lpart, s_logits, s_negmax, s_centred, s_exp, s_esum, s_inv, s_alpha = (
            sem("s_lpart"), sem("s_logits"), sem("s_negmax"), sem("s_centred"), sem("s_exp2"), sem("s_esum"),
            sem("s_inv2"), sem("s_alpha"))
        s_v, s_gated = sem("s_v"), sem("s_gated")
        s_y, s_yadd = [sem(f"s_y{b}") for b in range(2)], sem("s_yadd")
        s_res, s_out = ([sem(f"{n}{b}") for b in range(4)] for n in ("s_res", "s_out"))

        block = stack.enter_context(nc.Block())

        def over_groups(eng, slot):
            slot(0, True, False)
            with eng.Fori(1, groups - 1) as g:
                slot(g, False, False)
            slot(groups - 1, False, True)

        LEAD = 2 * GT

        def next_n(k):
            return [("n", k, 0), ("n", k, 1)]

        def units_of(last):
            beside = {"v1": next_n(0), "v2": next_n(1), "v3": [("g", 0, 0)] + next_n(2),
                      "u0": [("g", 1, 0)] + next_n(3), "u1": [("g", 2, 0)], "u2": [("g", 3, 0)]}
            if last:
                beside = {stage: [u for u in units if u[0] == "g"] for stage, units in beside.items()}
            number, numbered = 0, {}
            for stage, units in beside.items():
                numbered[stage] = [(number + i, *u) for i, u in enumerate(units)]
                number += len(units)
            return numbered

        UNITS = 3 * GT
        STATISTICS_AT = (1, 2, 4, 5)

        cols = [slice(e * P, (e + 1) * P) for e in range(KB)]
        chunks = [(w1_raw[:, :, c], w1_hi[:, :, c], w1_lo[:, :, c]) for c in cols]
        chunks += [(v_raw[:, k:k + 2, :], v_hi[:, k:k + 2, :], v_lo[:, k:k + 2, :]) for k in range(0, KB, 2)]
        v_ready = len(chunks)
        chunks += [(u_raw[:, k, :], u_hi[:, k, :], u_lo[:, k, :]) for k in range(RB)]

        def chunks_at(e):
            return range(2 * e + 1, min(2 * e + 3, len(chunks)))

        @block.sync
        def _(sp):
            def load(t, b):
                sp.dma_start(x_in[b][:], x1[bass.ts(t, P), :]).then_inc(s_xin[b], 16)

            def load_residual(g, i):
                b = i % 4
                if not (isinstance(g, int) and g == 0 and i < 4):
                    sp.wait_ge(s_out[b], g * 32 + (i // 4) * 16)
                sp.dma_start(result[b][:], x1[bass.ts(g * GT + i // 2, P), i % 2 * BANK:(i % 2 + 1) * BANK]
                             ).then_inc(s_res[b], 16)

            def store(g, i):
                sp.wait_ge(s_yadd, g * (2 * GT) + (i + 1))
                sp.dma_start(out[bass.ts(g * GT + i // 2, P), i % 2 * BANK:(i % 2 + 1) * BANK],
                             result[i % 4][:]).then_inc(s_out[i % 4], 16)

            def slot(g, first, last):
                if not last:
                    for k in range(GT):
                        if first and k < 2:
                            sp.wait_ge(s_turn, LEAD)
                        else:
                            sp.wait_ge(s_normed, g * GT + (k - 1))
                        load(g * GT + (GT + k), k % 2)
                for i in range(4):
                    load_residual(g, i)
                store(g, 0)
                for i in range(1, 5):
                    store(g, i)
                    load_residual(g, i + 3)
                for i in range(5, 2 * GT):
                    store(g, i)

            sp.dma_start(u_raw[:], shared["u_dram"]).then_inc(s_u_in, 16)
            for s in shared["s_x1"]:
                sp.wait_ge(s, 16 * tiles)
            over_groups(sp, slot)
            for b in range(4):
                sp.wait_ge(s_out[b], groups * 32)

        @block.gpsimd
        def _(pool):
            def factor(g, k):
                pool.wait_ge(s_var, g * GT + (k + 1))
                nc.gpsimd.tensor_tensor(rstd[k][:], var_eps[k][:], minus_half[:], ALU.pow).then_inc(s_rstd, 1)

            def slot(g, first, last):
                if not last:
                    for k in range(GT):
                        factor(g, k)

            nc.gpsimd.memset(minus_half[:], -0.5).then_inc(s_const, 1)
            nc.gpsimd.memset(ident[:], 0.0).then_inc(s_const, 1)
            pool.wait_ge(s_const, 2)
            nc.gpsimd.affine_select(out=ident[:], in_=ident[:], compare_op=ALU.not_equal, fill=1.0, base=0,
                                    pattern=[[-1, P]], channel_multiplier=1).then_inc(s_const, 1)
            over_groups(pool, slot)

        @block.scalar
        def _(act):
            def split_weights(n):
                raw, hi, lo = chunks[n]
                if n == v_ready:
                    act.wait_ge(s_u_in, 16)
                nc.scalar.activation(hi, raw, ACT.Copy).then_inc(s_whi, 1)

            def high_hidden(g, e):
                act.wait_ge(s_hidden, g * KB + (e + 1))
                if not (isinstance(g, int) and g == 0 and e < 2):
                    act.wait_ge(s_route, g * KB + (e - 1))
                nc.scalar.activation(hidden[e % 2][:], work[e % 2][:], ACT.Relu,
                                     bias=b1_col[:, e:e + 1]).then_inc(s_relu, 1)
                act.wait_ge(s_relu, g * KB + (e + 1))
                nc.scalar.activation(ht_hi[e % 2][:], hidden[e % 2][:], ACT.Copy).then_inc(s_hhi, 1)

            def high_unit(g, number, what, k, c, used):
                act.wait_ge(s_turn, g * UNITS + (LEAD + number + 1))
                if used is not None:
                    act.wait_ge(s_v if what == "n" else s_y[1], used)
                dst = nt_hi[:, 4 * c:4 * c + 4, k * P:(k + 1) * P] if what == "n" else gt_hi[k % 2][:]
                nc.scalar.activation(dst, turned[number % 2][:], ACT.Copy).then_inc(s_hi, 1)

            def slot(g, first, last):
                for e in range(KB):
                    if first:
                        for n in chunks_at(e):
                            split_weights(n)
                    high_hidden(g, e)
                act.wait_ge(s_route, g * KB + KB)
                nc.scalar.activation(logits_t[:], lt_ps[0:2 * E, :], ACT.Copy).then_inc(s_lt_out, 1)
                act.wait_ge(s_centred, g + 1)
                nc.scalar.activation(e_logits[:], centred[:], ACT.Exp).then_inc(s_exp, 1)
                for stage, units in units_of(last).items():
                    for number, what, k, c in units:
                        if what == "n":
                            used = g * GT + (k + 1)
                        else:
                            used = None if (first and k < 2) else g * GT + (k - 1)
                        high_unit(g, number, what, k, c, used)

            nc.scalar.activation(w2_both[:, :, 0:E], w2_raw[:], ACT.Copy).then_inc(s_w2, 1)
            split_weights(0)
            for n in range(LEAD):
                high_unit(-1, n - LEAD + UNITS, "n", n // 2, n % 2, None)
            over_groups(act, slot)

        @block.tensor
        def _(pe):
            mm = nc.tensor.matmul

            def hidden_products(g, e):
                def product(k, i):
                    if k == 0 and i == 0:
                        if e == 0:
                            pe.wait_ge(s_lo, g * UNITS + LEAD)
                        if isinstance(g, int) and g == 0:
                            pe.wait_ge(s_wlo, e + 1)
                        if e >= 2:
                            pe.wait_ge(s_relu, g * KB + (e - 1))
                        elif not (isinstance(g, int) and g == 0):
                            pe.wait_ge(s_gated, g * GT + (e - 1))
                    w, n = ((w1_hi, nt_hi), (w1_lo, nt_hi), (w1_hi, nt_lo))[i]
                    ins = mm(work[e % 2][:], w[:, k, cols[e]], n[:, k, :], start=(k == 0 and i == 0),
                             stop=(k == KB - 1 and i == 2))
                    if k == KB - 1 and i == 2:
                        ins.then_inc(s_hidden, 1)
                return [lambda k=k, i=i: product(k, i) for k in range(KB) for i in range(3)]

            def router_products(g, e):
                def product(i):
                    if i == 0:
                        pe.wait_ge(s_hlo, g * KB + (e + 1))
                        if e == 0 and isinstance(g, int) and g == 0:
                            pe.wait_ge(s_w2, 2)
                        elif e == 0:
                            pe.wait_ge(s_lt_out, g)
                        mm(lt_ps[0:2 * E, :], w2_both[:, e, :], ht_hi[e % 2][:], start=(e == 0),
                           stop=(e == KB - 1), skip_group_check=True)
                    else:
                        mm(lt_ps[0:E, :], w2_both[:, e, 0:E], ht_lo[e % 2][:], start=False,
                           stop=(e == KB - 1), skip_group_check=True).then_inc(s_route, 1)
                return [lambda i=i: product(i) for i in range(2)]

            def turn_logits(g):
                def turn(k):
                    ins = pe.transpose(l_ps[:, k, 0:2 * E], logits_t[:, k * P:(k + 1) * P],
                                       ident[0:2 * E, 0:2 * E])
                    if k == GT - 1:
                        ins.then_inc(s_l, 1)
                return [lambda k=k: turn(k) for k in range(GT)]

            def value_products(g, k):
                def product(d, i):
                    if d == 0 and i == 0:
                        if isinstance(g, int) and g == 0 and k == 0:
                            pe.wait_ge(s_wlo, v_ready)
                        if k < 2:
                            pe.wait_ge(s_relu, g * KB + (KB + k - 1))
                        else:
                            pe.wait_ge(s_gated, g * GT + (k - 1))
                    n, w = ((nt_hi, v_hi), (nt_hi, v_lo), (nt_lo, v_hi))[i]
                    ins = mm(work[k % 2][:], n[:, d, k * P:(k + 1) * P], w[:, d, :], start=(d == 0 and i == 0),
                             stop=(d == KB - 1 and i == 2))
                    if d == KB - 1 and i == 2:
                        ins.then_inc(s_v, 1)
                return [lambda d=d, i=i: product(d, i) for d in range(KB) for i in range(3)]

            def expert_products(g, k, unit):
                def product(c, r, i):
                    if r == 0 and i == 0:
                        if c == 0:
                            pe.wait_ge(s_lo, g * UNITS + (LEAD + unit + 1))
                            if isinstance(g, int) and g == 0 and k == 0:
                                pe.wait_ge(s_wlo, len(chunks))
                        if not (isinstance(g, int) and g == 0 and k == 0):
                            pe.wait_ge(s_yadd, g * (2 * GT) + (2 * k + c - 1))
                    w, u = ((gt_hi, u_hi), (gt_hi, u_lo), (gt_lo, u_hi))[i]
                    ins = mm(y_ps[c][:], w[k % 2][:, r, :], u[:, r, c * BANK:(c + 1) * BANK],
                             start=(r == 0 and i == 0), stop=(r == RB - 1 and i == 2))
                    if r == RB - 1 and i == 2:
                        ins.then_inc(s_y[c], 1)
                return [lambda c=c, r=r, i=i: product(c, r, i) for c in range(2) for r in range(RB)
                        for i in range(3)]

            def turn_unit(g, number, what, k, c):
                lead = isinstance(g, int) and g < 0

                def turn(i):
                    if i == 0:
                        if what == "n" and not lead:
                            pe.wait_ge(s_normed, g * GT + (k + 1))
                        elif what == "g":
                            pe.wait_ge(s_gated, g * GT + (k + 1))
                        if not (isinstance(g, int) and g * UNITS + LEAD + number < 2):
                            pe.wait_ge(s_lo, g * UNITS + (LEAD + number - 1))
                    n = first_n[k] if lead else normed[k % 2]
                    src = n[:, (4 * c + i) * P:(4 * c + i + 1) * P] if what == "n" else \
                        gated[k % 2][:, i * P:(i + 1) * P]
                    ins = pe.transpose(turned[number % 2][:, i, :], src, ident[:])
                    if i == 3:
                        ins.then_inc(s_turn, 1)
                return [lambda i=i: turn(i) for i in range(4)]

            def issue_all(functions):
                for issue in functions:
                    issue()

            def slot(g, first, last):
                beside = units_of(last)
                for e in range(KB):
                    big = hidden_products(g, e)
                    issue_all(big[:12] + (router_products(g, e - 1) if e else []) + big[12:])

                def turns_at(stage):
                    return [turn for unit in beside.get(stage, []) for turn in turn_unit(g, *unit)]

                big = value_products(g, 0)
                issue_all(big[:12] + router_products(g, KB - 1) + big[12:20])
                pe.wait_ge(s_lt_out, g + 1)
                if not (isinstance(g, int) and g == 0):
                    pe.wait_ge(s_logits, g)
                issue_all(interleave(big[20:], turn_logits(g), 1, 2))
                for k in range(1, GT):
                    issue_all(interleave(value_products(g, k), turns_at(f"v{k}"), 4, 1))
                gated_unit = {k: number for units in beside.values() for number, what, k, c in units
                              if what == "g"}
                for k in range(GT):
                    issue_all(interleave(expert_products(g, k, gated_unit[k]), turns_at(f"u{k}"), 2, 1))

            pe.wait_ge(s_const, 3)
            for n in range(LEAD):
                issue_all(turn_unit(-1, n - LEAD + UNITS, "n", n // 2, n % 2))
            over_groups(pe, slot)

        @block.vector
        def _(dve):
            def statistics(g, k):
                b = k % 2
                dve.wait_ge(s_xin[b], g * 32 + (k // 2 * 16 + 16))
                for c in range(2):
                    nc.vector.bn_stats(stats[:, 6 * c:6 * c + 6],
                                       x_in[b][:, c * BANK:(c + 1) * BANK]).then_inc(s_stat, 1)

            def variance(g, k):
                nc.vector.bn_aggr(mean_var[k][:], stats[:]).then_inc(s_stats, 1)
                dve.wait_ge(s_stats, g * GT + (k + 1))
                nc.vector.tensor_scalar(var_eps[k][:], mean_var[k][:, 1:2], EPS, None, ALU.add).then_inc(s_var, 1)

            def normalise(g, k, turned_units):
                dve.wait_ge(s_rstd, g * GT + (k + 1))
                if turned_units is not None:
                    dve.wait_ge(s_turn, turned_units)
                nc.vector.tensor_scalar(normed[k % 2][:], x_in[k % 2][:], mean_var[k][:, 0:1], rstd[k][:],
                                        ALU.subtract, ALU.mult).then_inc(s_normed, 1)

            def low_hidden(g, e):
                dve.wait_ge(s_hhi, g * KB + (e + 1))
                nc.vector.tensor_tensor(ht_lo[e % 2][:], hidden[e % 2][:], as_f32(ht_hi[e % 2][:]),
                                        ALU.subtract).then_inc(s_hlo, 1)

            def low_unit(g, number, what, k, c):
                dve.wait_ge(s_hi, g * UNITS + (LEAD + number + 1))
                at = (slice(None), slice(4 * c, 4 * c + 4), slice(k * P, (k + 1) * P))
                hi, lo = (nt_hi[at], nt_lo[at]) if what == "n" else (gt_hi[k % 2][:], gt_lo[k % 2][:])
                nc.vector.tensor_tensor(lo, turned[number % 2][:], as_f32(hi), ALU.subtract).then_inc(s_lo, 1)

            def split_weights(n):
                raw, hi, lo = chunks[n]
                dve.wait_ge(s_whi, n + 1)
                nc.vector.tensor_tensor(lo, raw, as_f32(hi), ALU.subtract).then_inc(s_wlo, 1)

            def softmax(g):
                dve.wait_ge(s_l, g + 1)
                nc.vector.tensor_tensor(logit_part[:], l_ps[:, :, 0:E], b2_row[:].unsqueeze(1).to_broadcast([P, GT, E]),
                                        ALU.add).then_inc(s_lpart, 1)
                dve.wait_ge(s_lpart, g + 1)
                nc.vector.tensor_tensor(logits[:], l_ps[:, :, E:2 * E], logit_part[:], ALU.add).then_inc(s_logits, 1)
                dve.wait_ge(s_logits, g + 1)
                nc.vector.tensor_reduce(neg_max[:], logits[:], AX_X, ALU.max, negate=True).then_inc(s_negmax, 1)
                dve.wait_ge(s_negmax, g + 1)
                nc.vector.tensor_tensor(centred[:], logits[:], neg_max[:].unsqueeze(2).to_broadcast([P, GT, E]),
                                        ALU.add).then_inc(s_centred, 1)
                dve.wait_ge(s_exp, g + 1)
                nc.vector.tensor_reduce(e_sum[:], e_logits[:], AX_X, ALU.add).then_inc(s_esum, 1)
                dve.wait_ge(s_esum, g + 1)
                nc.vector.reciprocal(inv_sum[:], e_sum[:]).then_inc(s_inv, 1)
                dve.wait_ge(s_inv, g + 1)
                nc.vector.tensor_tensor(alpha[:], e_logits[:], inv_sum[:].unsqueeze(2).to_broadcast([P, GT, E]),
                                        ALU.mult).then_inc(s_alpha, 1)

            def gate(g, k, turned_units):
                dve.wait_ge(s_v, g * GT + (k + 1))
                if k == 0:
                    dve.wait_ge(s_alpha, g + 1)
                if turned_units is not None:
                    dve.wait_ge(s_turn, turned_units)
                nc.vector.tensor_tensor(gated[k % 2][:].rearrange("p (e r) -> p e r", e=E),
                                        work[k % 2][:].rearrange("p (e r) -> p e r", e=E),
                                        alpha[:, k, :].unsqueeze(2).to_broadcast([P, E, KR // E]),
                                        ALU.mult).then_inc(s_gated, 1)

            def add_residual(g, i):
                dve.wait_ge(s_y[i % 2], g * GT + (i // 2 + 1))
                dve.wait_ge(s_res[i % 4], g * 32 + (i // 4 * 16 + 16))
                nc.vector.tensor_tensor(result[i % 4][:], y_ps[i % 2][:], result[i % 4][:],
                                        ALU.add).then_inc(s_yadd, 1)

            def slot(g, first, last):
                beside = units_of(last)

                def turned_after(what, k):
                    number = max(n for units in beside.values() for n, w, tile, c in units if (w, tile) == (what, k))
                    return g * UNITS + (LEAD + number + 1)

                def low_units(stage):
                    for unit in beside.get(stage, []):
                        low_unit(g, *unit)

                for e in range(KB):
                    if first:
                        for n in chunks_at(e):
                            split_weights(n)
                    if e in STATISTICS_AT and not last:
                        k = STATISTICS_AT.index(e)
                        statistics(g, k)
                        dve.wait_ge(s_stat, g * (2 * GT) + (2 * k + 2))
                    low_hidden(g, e)
                    if e in STATISTICS_AT and not last:
                        variance(g, k)
                        if k < 2:
                            normalise(g, k, g * UNITS + LEAD)
                softmax(g)
                gate(g, 0, None if first else g * UNITS + LEAD)
                low_units("v1")
                gate(g, 1, None if first else g * UNITS + LEAD)
                low_units("v2")
                if not last:
                    normalise(g, 2, turned_after("n", 0))
                gate(g, 2, turned_after("g", 0))
                low_units("v3")
                if not last:
                    normalise(g, 3, turned_after("n", 1))
                gate(g, 3, turned_after("g", 1))
                for k in range(GT):
                    low_units(f"u{k}")
                    add_residual(g, 2 * k)
                    add_residual(g, 2 * k + 1)

            dve.wait_ge(s_w2, 1)
            nc.vector.tensor_tensor(w2_both[:, :, E:2 * E], w2_raw[:], as_f32(w2_both[:, :, 0:E]),
                                    ALU.subtract).then_inc(s_w2, 1)
            for k in range(GT):
                for c in range(2):
                    low_unit(-1, UNITS - LEAD + 2 * k + c, "n", k, c)
                if k == 0:
                    split_weights(0)
            over_groups(dve, slot)


def cross_attention_and_mixture(nc, x, ctx, ctx_t, gamma, u_t, v_t, w1, b1_t, w2, b2, out):
    D, KR = v_t.shape
    E = w2.shape[1]
    KB, RB = D // P, KR // P
    x1 = nc.dram_tensor("x1", tuple(x.shape), F32, kind="Internal").ap()
    scratch = nc.dram_tensor("gains", (2 * x.shape[0] // P, BANK), F32, kind="Internal").ap()

    place = SbufMap(nc, (nc.sbuf_base + 31) // 32 * 32)
    shared = {
        "w2_raw": place.tensor("w2_raw", [P, KB, E]),
        "b1_col": place.tensor("b1_col", [P, KB]),
        "b2_row": place.tensor("b2_row", [P, E]),
    }
    low = SbufMap(nc, place.at)
    for name, blocks, width in (("w1", KB, D), ("v", KB, KR), ("u", RB, D)):
        if name == "u":
            shared["loaded_end"] = place.at
        shared[name + "_raw"] = place.tensor(name + "_raw", [P, blocks, width])
        shared[name + "_lo"] = low.tensor(name + "_lo", [P, blocks, width], F32R)
    shared["w1_hi"] = place.tensor("w1_hi", [P, KB, D], F32R)
    shared["v_hi"] = place.tensor("v_hi", [P, KB, KR], F32R)
    shared["first_at"] = place.at
    shared["first_n"] = [place.tensor(f"first_n{k}", [P, D]) for k in range(FIRST)]
    shared["u_hi"] = place.tensor("u_hi", [P, RB, D], F32R)
    shared["end"] = place.at
    shared["top_at"] = nc.sbuf_usable_end // 32 * 32 - 4 * BANK * 4

    w1_rows, v_rows = (a.rearrange("(k p) n -> p k n", p=P) for a in (w1, v_t))
    shared["loads"] = [(shared["w2_raw"][:], w2.rearrange("(k p) e -> p k e", p=P)),
                       (shared["b1_col"][:], b1_t),
                       (shared["b2_row"][:], b2.partition_broadcast(P))]
    shared["loads"] += [(shared["w1_raw"][:, k, :], w1_rows[:, k, :]) for k in range(KB)]
    shared["loads"] += [(shared["v_raw"][:, k:k + 2, :], v_rows[:, k:k + 2, :]) for k in range(0, KB, 2)]
    shared["u_dram"] = u_t.rearrange("(k p) d -> p k d", p=P)
    with ExitStack() as stack:
        shared["s_x1"] = [stack.enter_context(nc.semaphore(f"s_x1{b}")) for b in range(2)]
        attention(nc, x, ctx, ctx_t, gamma, x1, scratch, shared)
        mixture(nc, x1, shared, out)


def kernel(**inputs):
    import numpy as np
    import concourse.bacc as bacc
    from concourse.bass_utils import run_bass_kernel_spmd

    x = np.asarray(inputs["x"])
    ctx = np.asarray(inputs["ctx_2048"])
    B, S, D = x.shape
    heads = B * S // P
    U, V = np.asarray(inputs["L0_ffn_U"]), np.asarray(inputs["L0_ffn_V"])
    experts, _, rank = U.shape
    ctx_t = ctx.reshape(heads, P, D // P, P).transpose(0, 3, 2, 1)
    arrays = {
        "x": x.reshape(B * S, D),
        "ctx": ctx.reshape(B * S, D),
        "ctx_t": ctx_t.reshape(B * S, D),
        "gamma": np.asarray(inputs["L0_xattn_gamma"]).reshape(1, 1),
        "u_t": U.transpose(0, 2, 1).reshape(experts * rank, D),
        "v_t": V.reshape(experts * rank, D).transpose(1, 0),
        "w1": np.asarray(inputs["L0_ffn_W1"]),
        "b1_t": np.asarray(inputs["L0_ffn_b1"]).reshape(D // P, P).transpose(1, 0),
        "w2": np.asarray(inputs["L0_ffn_W2"]),
        "b2": np.asarray(inputs["L0_ffn_b2"]),
    }
    arrays = {"in_" + name: np.ascontiguousarray(a) for name, a in arrays.items()}
    nc = bacc.Bacc("TRN2", target_bir_lowering=False, num_devices=1)
    args = [nc.dram_tensor(name, a.shape, mybir.dt.from_np(a.dtype), kind="ExternalInput").ap()
            for name, a in arrays.items()]
    args.append(nc.dram_tensor("out", (B * S, D), F32, kind="ExternalOutput").ap())
    cross_attention_and_mixture(nc, *args)
    result = run_bass_kernel_spmd(nc, [arrays], core_ids=[0])
    return result.results[0]["out"].reshape(B, S, D)
```

```python
from contextlib import ExitStack

import concourse.bass as bass
from concourse import mybir

F32 = mybir.dt.float32
F32R = mybir.dt.float32r
ALU = mybir.AluOpType
ACT = mybir.ActivationFunctionType
AX_X = mybir.AxisListType.X

P = 128
BANK = 512
FIRST = 4
EPS = 1e-5


class SbufMap:

    def __init__(self, nc, offset):
        self.nc, self.at = nc, offset

    def tensor(self, name, shape, dtype=F32):
        size = 4
        for n in shape[1:]:
            size *= n
        got = self.nc.alloc_sbuf_tensor_at(name, shape, dtype, offset=self.at)
        self.at += (size + 31) // 32 * 32
        assert self.at <= self.nc.sbuf_usable_end, name
        return got


def as_f32(tile):
    return tile.bitcast(F32)


def interleave(big, small, lead, rate):
    big, small = list(big), list(small)
    order = big[:lead]
    del big[:lead]
    while big or small:
        order += small[:rate]
        del small[:rate]
        order += big[:1]
        del big[:1]
    return order


def attention(nc, sem, x, ctx, ctx_t, gamma, x1, scratch, shared):
    rows, L = x.shape
    heads = rows // P
    JB = L // P
    HALF = JB // 2
    assert L == 2 * BANK and HALF * P == BANK

    place = SbufMap(nc, shared["loaded_end"])
    pt_hi, pt_lo = [], []
    for b in range(2):
        pt_hi.append(place.tensor(f"pt_hi{b}", [P, JB, BANK], F32R))
        pt_lo.append(place.tensor(f"pt_lo{b}", [P, JB, BANK], F32R))
    assert place.at == shared["first_at"]
    q_hi, q_lo, k_hi, k_lo = ([place.tensor(f"{name}0", [P, L], F32R)] for name in ("q_hi", "q_lo", "k_hi", "k_lo"))
    for name, tiles in (("q_hi", q_hi), ("q_lo", q_lo), ("k_hi", k_hi), ("k_lo", k_lo)):
        tiles.append(place.tensor(f"{name}1", [P, L], F32R))
    assert place.at == shared["nt_at"] + 4 * L * 4
    x_raw = place.tensor("x_raw", [P, L])
    k_raw = place.tensor("k_raw", [P, L])
    v_raw = place.tensor("v_raw", [P, JB, P])
    q32 = place.tensor("q32", [P, L])
    v_hi = [place.tensor(f"v_hi{b}", [P, JB, P], F32R) for b in range(2)]
    v_lo = [place.tensor(f"v_lo{b}", [P, JB, P], F32R) for b in range(2)]
    x_res = place.tensor("x_res", [P, L])
    probs = [place.tensor(f"probs{b}", [P, L]) for b in range(2)]
    gain_row = [place.tensor(f"gain_row{b}", [P, BANK]) for b in range(2)]
    scaled = [place.tensor(f"scaled{b}", [P, BANK]) for b in range(2)]
    top = SbufMap(nc, shared["top_at"])
    x1_out = [top.tensor(f"x1_out{b}", [P, BANK]) for b in range(2)]
    first_mean_var = [place.tensor(f"first_mean_var{k}", [P, 2]) for k in range(FIRST)]
    first_var_eps = [place.tensor(f"first_var_eps{k}", [P, 1]) for k in range(FIRST)]
    first_rstd = [place.tensor(f"first_rstd{k}", [P, 1]) for k in range(FIRST)]
    gamma_col = place.tensor("gamma_col", [P, 1])
    stats = [place.tensor(f"stats{b}", [P, 12]) for b in range(2)]
    mean_var = [place.tensor(f"mean_var{b}", [P, 2]) for b in range(2)]
    var_scaled = [place.tensor(f"var_scaled{b}", [P, 1]) for b in range(2)]
    q_scale = [place.tensor(f"q_scale{b}", [P, 1]) for b in range(2)]
    neg_max = place.tensor("neg_max", [P, JB])
    row_sum = [place.tensor(f"row_sum{b}", [P, JB]) for b in range(2)]
    inv_sum = [place.tensor(f"inv_sum{b}", [P, HALF]) for b in range(2)]
    gain = [place.tensor(f"gain{b}", [P, HALF]) for b in range(2)]

    assert place.at <= shared["top_at"]

    ident, minus_half, zero_col = shared["ident"], shared["minus_half"], shared["zero_col"]
    scores, turned0, turned1, attended = shared["scores"], shared["turned0"], shared["turned1"], shared["attended"]
    first_turned = shared["turned"]

    s_gamma = sem("s_gamma")
    s_x_in, s_k_in, s_v_in, s_res_in = sem("s_x_in"), sem("s_k_in"), sem("s_v_in"), sem("s_res_in")
    s_pre = shared["s_pre"]
    s_stat, s_stats, s_var, s_qscale, s_q32 = (sem("s_stat"), sem("s_stats"), sem("s_var"), sem("s_qscale"),
                                               sem("s_q32"))
    s_qhi, s_qlo, s_ksplit, s_vsplit = sem("s_qhi"), sem("s_qlo"), sem("s_ksplit"), sem("s_vsplit")
    s_scores, s_max, s_exp = sem("s_scores"), sem("s_max"), sem("s_exp")
    s_turn0, s_turn1 = sem("s_turn0"), sem("s_turn1")
    s_hi0, s_hi1, s_lo0, s_lo1 = sem("s_hi0"), sem("s_hi1"), sem("s_lo0"), sem("s_lo1")
    s_pv = shared["s_pv"]
    s_inv, s_gain, s_gain_out = sem("s_inv"), sem("s_gain"), sem("s_gain_out")
    s_gain_in, s_scaled, s_added = sem("s_gain_in"), sem("s_scaled"), shared["s_added"]
    s_x1, s_const = shared["s_x1"], shared["s_const"]
    s_f_in = [sem(f"s_f_in{k}") for k in range(FIRST)]
    s_f_stat, s_f_stats, s_f_var, s_f_rstd = sem("s_f_stat"), sem("s_f_stats"), sem("s_f_var"), sem("s_f_rstd")
    s_f_n = [sem(f"s_f_n{k}") for k in range(FIRST)]
    s_turn, s_hi, s_lo = shared["s_turn"], shared["s_hi"], shared["s_lo"]
    s_w_first = shared["s_w_first"]
    first_n = shared["first_n"]

    def first_place(u):
        return slice(None), slice(u % 2 * 4, u % 2 * 4 + 4), slice(u // 2 * P, (u // 2 + 1) * P)

    def over_heads(eng, slot):
        slot(0, 0, 0, True, False)
        slot(1, JB, 1, False, False)
        with eng.Fori(1, heads // 2 - 1) as pair:
            slot(pair * 2, pair * (2 * JB), 0, False, False)
            slot(pair * 2 + 1, pair * (2 * JB) + JB, 1, False, False)
        slot(heads - 2, (heads - 2) * JB, 0, False, False)
        slot(heads - 1, (heads - 1) * JB, 1, False, True)
        return heads, heads * JB

    def sync(sp):
        def rows_of(h):
            return bass.ts(h, P)

        def load_x(h):
            sp.dma_start(x_raw[:], x[rows_of(h), :]).then_inc(s_x_in, 16)

        def load_k(h):
            sp.dma_start(k_raw[:], ctx[rows_of(h), :]).then_inc(s_k_in, 16)

        def load_v(h):
            sp.dma_start(v_raw[:], ctx_t[rows_of(h), :].rearrange("p (b d) -> p b d", d=P)).then_inc(s_v_in, 16)

        def load_residual(h):
            sp.dma_start(x_res[:], x[rows_of(h), :]).then_inc(s_res_in, 16)

        def spread_gain(half, b):
            sp.wait_ge(s_gain, half + 1)
            sp.dma_start(scratch[bass.ds(half, 1), :].rearrange("a (p j) -> (a p) j", p=P),
                         gain[b][:]).then_inc(s_gain_out, 16)
            sp.wait_ge(s_gain_out, half * 16 + 16)
            sp.dma_start(gain_row[b][:], scratch[bass.ds(half, 1), :].rearrange("a n -> (a n)")
                         .partition_broadcast(P)).then_inc(s_gain_in, 16)

        def store_x1(h, b):
            sp.wait_ge(s_added, h * 2 + b + 1)
            sp.dma_start(x1[rows_of(h), b * BANK:(b + 1) * BANK], x1_out[b][:]).then_inc(s_x1[b], 16)

        def load_first(n):
            sp.wait_ge(s_scores, n)
            for b in range(2):
                sp.wait_ge(s_x1[b], 16 * len(first_n))
            for k, tile in enumerate(first_n):
                sp.dma_start(tile[:], x1[bass.ts(k, P), :]).then_inc(s_f_in[k], 16)

        def preload_weights(count):
            for tile, dram in loads[:count]:
                sp.dma_start(tile, dram).then_inc(s_pre, 16)
            del loads[:count]

        loads = list(shared["loads"])

        def slot(h, n, parity, first, last):
            early = isinstance(h, int) and h < 2
            more = not (isinstance(h, int) and h + 2 >= heads)
            if last:
                load_first(n)
            if not first:
                spread_gain(h * 2 - 1, 1)
            if not last:
                sp.wait_ge(s_vsplit, h * 2 + 2)
                load_v(h + 1)
            if not first:
                store_x1(h - 1, 0)
            if early and not first:
                preload_weights(4)
            if more:
                sp.wait_ge(s_ksplit, h * 2 + 4)
                load_k(h + 2)
                sp.wait_ge(s_q32, h + 2)
                load_x(h + 2)
            spread_gain(h * 2, 0)
            if not first:
                store_x1(h - 1, 1)
                load_residual(h)
            if early:
                preload_weights(6 if first else 5)

        load_x(0)
        load_k(0)
        sp.dma_start(gamma_col[:], gamma.rearrange("a b -> (a b)").partition_broadcast(P)).then_inc(s_gamma, 16)
        load_v(0)
        load_residual(0)
        sp.wait_ge(s_q32, 1)
        load_x(1)
        sp.wait_ge(s_ksplit, 2)
        load_k(1)
        h, _ = over_heads(sp, slot)
        spread_gain(2 * h - 1, 1)
        store_x1(h - 1, 0)
        store_x1(h - 1, 1)

    def gpsimd(pool):
        def scale_of_queries(h, b):
            pool.wait_ge(s_var, h + 1)
            nc.gpsimd.tensor_tensor(q_scale[b][:], var_scaled[b][:], minus_half[:], ALU.pow).then_inc(s_qscale, 1)

        def split_keys(h, n, b):
            pool.wait_ge(s_k_in, h * 16 + 16)
            if not (isinstance(h, int) and h < 2):
                pool.wait_ge(s_scores, n - JB)
            nc.gpsimd.tensor_tensor(k_hi[b][:], k_raw[:], zero_col[:].to_broadcast([P, L]), ALU.add).then_inc(s_ksplit, 1)
            pool.wait_ge(s_ksplit, h * 2 + 1)
            nc.gpsimd.tensor_tensor(k_lo[b][:], k_raw[:], as_f32(k_hi[b][:]), ALU.subtract).then_inc(s_ksplit, 1)

        def split_values(h, n, b):
            pool.wait_ge(s_v_in, h * 16 + 16)
            if not (isinstance(h, int) and h < 2):
                pool.wait_ge(s_pv, n - JB)
            nc.gpsimd.tensor_tensor(v_hi[b][:], v_raw[:], zero_col[:].unsqueeze(2).to_broadcast([P, JB, P]),
                                    ALU.add).then_inc(s_vsplit, 1)
            pool.wait_ge(s_vsplit, h * 2 + 1)
            nc.gpsimd.tensor_tensor(v_lo[b][:], v_raw[:], as_f32(v_hi[b][:]), ALU.subtract).then_inc(s_vsplit, 1)

        def low_queries(h, b):
            pool.wait_ge(s_qhi, h + 1)
            nc.gpsimd.tensor_tensor(q_lo[b][:], q32[:], as_f32(q_hi[b][:]), ALU.subtract).then_inc(s_qlo, 1)

        def add_residual(h, b):
            pool.wait_ge(s_scaled, h * 2 + b + 1)
            if b == 0:
                pool.wait_ge(s_res_in, h * 16 + 16)
            if not (isinstance(h, int) and h == 0):
                pool.wait_ge(s_x1[b], h * 16)
            nc.gpsimd.tensor_tensor(x1_out[b][:], x_res[:, b * BANK:(b + 1) * BANK], scaled[b][:],
                                    ALU.add).then_inc(s_added, 1)

        def first_factor(k):
            pool.wait_ge(s_f_var, k + 1)
            nc.gpsimd.tensor_tensor(first_rstd[k][:], first_var_eps[k][:], minus_half[:], ALU.pow).then_inc(s_f_rstd, 1)

        def normalise_first(k):
            pool.wait_ge(s_f_rstd, k + 1)
            nc.gpsimd.tensor_scalar(first_n[k][:], first_n[k][:], first_mean_var[k][:, 0:1], first_rstd[k][:],
                                    ALU.subtract, ALU.mult).then_inc(s_f_n[k], 1)

        def split_first_weights(n):
            raw, hi, lo = shared["first_weights"]
            pool.wait_ge(s_pre, 16 * len(shared["loads"]))
            pool.wait_ge(s_pv, n - 4)
            nc.gpsimd.tensor_tensor(hi, raw, zero_col[:].unsqueeze(2).to_broadcast([P, JB, P]), ALU.add).then_inc(s_w_first, 1)
            pool.wait_ge(s_w_first, 1)
            nc.gpsimd.tensor_tensor(lo, raw, as_f32(hi), ALU.subtract).then_inc(s_w_first, 1)

        def slot(h, n, parity, first, last):
            split_values(h, n, parity)
            if not first:
                add_residual(h - 1, 0)
            if last:
                first_factor(0)
                normalise_first(0)
                first_factor(1)
                first_factor(2)
            if not last:
                scale_of_queries(h + 1, 1 - parity)
                split_keys(h + 1, n + JB, 1 - parity)
                low_queries(h + 1, 1 - parity)
            if not first:
                add_residual(h - 1, 1)

        nc.gpsimd.memset(minus_half[:], -0.5).then_inc(s_const, 1)
        nc.gpsimd.memset(zero_col[:], 0.0).then_inc(s_const, 1)
        nc.gpsimd.memset(ident[:], 0.0).then_inc(s_const, 1)
        pool.wait_ge(s_const, 3)
        nc.gpsimd.affine_select(out=ident[:], in_=ident[:], compare_op=ALU.not_equal, fill=1.0, base=0,
                                pattern=[[-1, P]], channel_multiplier=1).then_inc(s_const, 1)
        scale_of_queries(0, 0)
        pool.wait_ge(s_ksplit, 1)
        nc.gpsimd.tensor_tensor(k_lo[0][:], k_raw[:], as_f32(k_hi[0][:]), ALU.subtract).then_inc(s_ksplit, 1)
        h, n = over_heads(pool, slot)
        first_factor(3)
        split_first_weights(n)
        add_residual(h - 1, 0)
        add_residual(h - 1, 1)

    def scalar(act):
        def high_probs(t, j, n, part, early):
            s_turn, s_hi = (s_turn0, s_hi0) if part == 0 else (s_turn1, s_hi1)
            half = j // HALF
            act.wait_ge(s_turn, t + 1)
            if j % HALF == 0 and not early:
                act.wait_ge(s_pv, n - JB + 4 * half + (2 if part == 0 else 4))
            src = turned0 if part == 0 else turned1[j % 2]
            col = j % HALF * P
            nc.scalar.activation(pt_hi[half][:, 4 * part:4 * part + 4, col:col + P], src[:],
                                 ACT.Copy).then_inc(s_hi, 1)

        def exps(s, j, b):
            act.wait_ge(s_max, s + 1)
            nc.scalar.activation(probs[j % 2][:], scores[j % 2][:], ACT.Exp, bias=neg_max[:, j:j + 1],
                                 accum_out=row_sum[b][:, j:j + 1]).then_inc(s_exp, 1)

        def high_queries(h, n, b):
            act.wait_ge(s_q32, h + 1)
            if not (isinstance(h, int) and h < 2):
                act.wait_ge(s_scores, n - JB)
            nc.scalar.activation(q_hi[b][:], q32[:], ACT.Copy).then_inc(s_qhi, 1)

        def slot(h, n, parity, first, last):
            for j in range(JB):
                back = (n + j - 1, (j - 1) % JB, n if j else n - JB)
                early = first or (j == 0 and isinstance(h, int) and h == 1)
                if not (first and j == 0):
                    high_probs(*back, 0, early)
                exps(n + j, j, parity)
                if not (first and j == 0):
                    high_probs(*back, 1, early)
                if j == 5 and not last:
                    high_queries(h + 1, n + JB, 1 - parity)

        act.wait_ge(s_k_in, 16)
        nc.scalar.activation(k_hi[0][:], k_raw[:], ACT.Copy).then_inc(s_ksplit, 1)
        high_queries(0, 0, 0)
        h, n = over_heads(act, slot)
        for part in range(2):
            high_probs(n - 1, JB - 1, n - JB, part, False)
        for u in range(2 * FIRST):
            act.wait_ge(s_turn, u + 1)
            nc.scalar.activation(shared["nt_hi"][first_place(u)], first_turned[u % 2], ACT.Copy).then_inc(s_hi, 1)

    def tensor(pe):
        mm = nc.tensor.matmul

        def score_products(s, j, h, b):
            if not (isinstance(s, int) and s < 2):
                pe.wait_ge(s_exp, s - 1)
            queries = slice(j * P, (j + 1) * P)
            for i, (q, k) in enumerate(((q_hi, k_hi), (q_hi, k_lo), (q_lo, k_hi))):
                if j == 0 and i == 0:
                    pe.wait_ge(s_qhi, h + 1)
                    pe.wait_ge(s_ksplit, h * 2 + 1)
                elif j == 0 and i == 1:
                    pe.wait_ge(s_ksplit, h * 2 + 2)
                elif j == 0:
                    pe.wait_ge(s_qlo, h + 1)
                for c in range(2):
                    last = mm(scores[j % 2][:, c * BANK:(c + 1) * BANK], q[b][:, queries],
                              k[b][:, c * BANK:(c + 1) * BANK], start=(i == 0), stop=(i == 2))
            last.then_inc(s_scores, 1)

        def turns(t, j):
            def turn(i):
                if i == 0:
                    pe.wait_ge(s_exp, t + 1)
                    if not (isinstance(t, int) and t < 1):
                        pe.wait_ge(s_lo0, t)
                if i == 4 and not (isinstance(t, int) and t < 2):
                    pe.wait_ge(s_lo1, t - 1)
                dst = turned0 if i < 4 else turned1[j % 2]
                ins = pe.transpose(dst[:, i % 4, :], probs[j % 2][:, i * P:(i + 1) * P], ident[:])
                if i == 3:
                    ins.then_inc(s_turn0, 1)
                if i == 7:
                    ins.then_inc(s_turn1, 1)
            return [lambda i=i: turn(i) for i in range(JB)]

        def attended_products(h, n, half, quarter, b):
            def product(i):
                if i == 0 and quarter == 0:
                    pe.wait_ge(s_lo0, n + 4 * half + 4)
                    pe.wait_ge(s_lo1, n + 4 * half + 4)
                    if half == 0:
                        pe.wait_ge(s_vsplit, h * 2 + 2)
                    if not (isinstance(h, int) and h == 0 and half == 0):
                        pe.wait_ge(s_scaled, h * 2 + half)
                lb = 2 * quarter + i // 3
                v, pt = ((v_hi, pt_hi), (v_hi, pt_lo), (v_lo, pt_hi))[i % 3]
                ins = mm(attended[:], v[b][:, lb, :], pt[half][:, lb, :],
                         start=(quarter == 0 and i == 0), stop=(quarter == 3 and i == 5))
                if i == 5:
                    ins.then_inc(s_pv, 1)
            return [lambda i=i: product(i) for i in range(6)]

        def quarter_at(h, n, j, parity, first):
            if j >= 6:
                return attended_products(h, n, 0, j - 6, parity)
            if first:
                return []
            if j < 2:
                return attended_products(h - 1, n - JB, 0, j + 2, 1 - parity)
            return attended_products(h - 1, n - JB, 1, j - 2, 1 - parity)

        def turn_first(u):
            def turn(i):
                if i == 0:
                    pe.wait_ge(s_f_n[u // 2], 1)
                    if u == 0:
                        pe.wait_ge(s_exp, heads * JB)
                    elif u >= 2:
                        pe.wait_ge(s_lo, u - 1)
                block = u % 2 * 4 + i
                ins = pe.transpose(first_turned[u % 2][:, i, :], first_n[u // 2][:, block * P:(block + 1) * P], ident[:])
                if i == 3:
                    ins.then_inc(s_turn, 1)
            return [lambda i=i: turn(i) for i in range(4)]

        def slot(h, n, parity, first, last):
            for j in range(JB):
                score_products(n + j, j, h, parity)
                small = [] if first and j == 0 else turns(n + j - 1, (j - 1) % JB)
                for issue in interleave(quarter_at(h, n, j, parity, first), small, 0, 2):
                    issue()

        pe.wait_ge(s_const, 4)
        h, n = over_heads(pe, slot)
        for j in range(6):
            small = turns(n - 1, JB - 1) if j == 0 else turn_first(2 * j - 2) + turn_first(2 * j - 1) if j < 5 else []
            for issue in interleave(quarter_at(h, n, j, 0, False), small, 0, 2):
                issue()

    def vector(dve):
        def maxima(s, j):
            dve.wait_ge(s_scores, s + 1)
            nc.vector.tensor_reduce(neg_max[:, j:j + 1], scores[j % 2][:], AX_X, ALU.max,
                                    negate=True).then_inc(s_max, 1)

        def low_probs(t, j, part):
            s_hi, s_lo = (s_hi0, s_lo0) if part == 0 else (s_hi1, s_lo1)
            half, col = j // HALF, j % HALF * P
            dve.wait_ge(s_hi, t + 1)
            src = turned0 if part == 0 else turned1[j % 2]
            at = (slice(None), slice(4 * part, 4 * part + 4), slice(col, col + P))
            nc.vector.tensor_tensor(pt_lo[half][at], src[:], as_f32(pt_hi[half][at]),
                                    ALU.subtract).then_inc(s_lo, 1)

        def statistics(h, b, c):
            if c == 0:
                dve.wait_ge(s_x_in, h * 16 + 16)
            nc.vector.bn_stats(stats[b][:, 6 * c:6 * c + 6],
                               x_raw[:, c * BANK:(c + 1) * BANK]).then_inc(s_stat, 1)

        def variance(h, b):
            nc.vector.bn_aggr(mean_var[b][:], stats[b][:]).then_inc(s_stats, 1)
            dve.wait_ge(s_stats, h + 1)
            nc.vector.tensor_scalar(var_scaled[b][:], mean_var[b][:, 1:2], EPS, float(P),
                                    ALU.add, ALU.mult).then_inc(s_var, 1)

        def queries(h, b):
            dve.wait_ge(s_qscale, h + 1)
            if not (isinstance(h, int) and h == 0):
                dve.wait_ge(s_qlo, h)
            nc.vector.tensor_scalar(q32[:], x_raw[:], mean_var[b][:, 0:1], q_scale[b][:],
                                    ALU.subtract, ALU.mult).then_inc(s_q32, 1)

        def gains(h, half, b):
            number = h * 2 + half
            nc.vector.reciprocal(inv_sum[half][:], row_sum[b][:, half * HALF:(half + 1) * HALF]).then_inc(s_inv, 1)
            if not (isinstance(h, int) and h == 0):
                dve.wait_ge(s_gain_out, number * 16 - 16)
            else:
                dve.wait_ge(s_gamma, 16)
            dve.wait_ge(s_inv, number + 1)
            nc.vector.tensor_scalar(gain[half][:], inv_sum[half][:], gamma_col[:], None,
                                    ALU.mult).then_inc(s_gain, 1)

        def scale_attended(h, n, half):
            dve.wait_ge(s_pv, n + 4 * half + 4)
            dve.wait_ge(s_gain_in, h * 32 + (half * 16 + 16))
            if not (isinstance(h, int) and h == 0):
                dve.wait_ge(s_added, h * 2 + half - 1)
            nc.vector.tensor_tensor(scaled[half][:].rearrange("p (j a) -> p j a", j=HALF),
                                    attended[:].rearrange("p (j a) -> p j a", j=HALF),
                                    gain_row[half][:].rearrange("p (a j) -> p j a", j=HALF),
                                    ALU.mult).then_inc(s_scaled, 1)

        def first_statistics(part):
            k, c = part // 2, part % 2
            dve.wait_ge(s_f_in[k], 16)
            nc.vector.bn_stats(stats[k % 2][:, 6 * c:6 * c + 6],
                               first_n[k][:, c * BANK:(c + 1) * BANK]).then_inc(s_f_stat, 1)

        def first_variance(k):
            dve.wait_ge(s_f_stat, 2 * k + 2)
            nc.vector.bn_aggr(first_mean_var[k][:], stats[k % 2][:]).then_inc(s_f_stats, 1)
            dve.wait_ge(s_f_stats, k + 1)
            nc.vector.tensor_scalar(first_var_eps[k][:], first_mean_var[k][:, 1:2], EPS, None,
                                    ALU.add).then_inc(s_f_var, 1)

        def normalise_first(k):
            dve.wait_ge(s_f_rstd, k + 1)
            nc.vector.tensor_scalar(first_n[k][:], first_n[k][:], first_mean_var[k][:, 0:1], first_rstd[k][:],
                                    ALU.subtract, ALU.mult).then_inc(s_f_n[k], 1)

        def low_first(u):
            dve.wait_ge(s_hi, u + 1)
            at = first_place(u)
            nc.vector.tensor_tensor(shared["nt_lo"][at], first_turned[u % 2], as_f32(shared["nt_hi"][at]),
                                    ALU.subtract).then_inc(s_lo, 1)

        def slot(h, n, parity, first, last):
            for j in range(JB):
                s = n + j
                maxima(s, j)
                if j == 3 and not last:
                    dve.wait_ge(s_stat, h * 2 + 4)
                if not (first and j < 1):
                    low_probs(s - 1, (j - 1) % JB, 0)
                if not (first and j < 2):
                    low_probs(s - 2, (j - 2) % JB, 1)
                if j in (1, 5) and not first:
                    scale_attended(h - 1, n - JB, j // 4)
                if last and j > 0:
                    first_statistics(j - 1)
                    if j % 2 == 0:
                        first_variance(j // 2 - 1)
                    if j == 5:
                        normalise_first(1)
                    if j == 7:
                        first_statistics(JB - 1)
                        first_variance(FIRST - 1)
                if j in (0, 2) and not last:
                    statistics(h + 1, 1 - parity, j // 2)
                if j == 3 and not last:
                    variance(h + 1, 1 - parity)
                if j == 2 and not first:
                    gains(h - 1, 1, 1 - parity)
                if j == 4 and not last:
                    queries(h + 1, 1 - parity)
                if j == 6:
                    gains(h, 0, parity)

        statistics(0, 0, 0)
        statistics(0, 0, 1)
        dve.wait_ge(s_stat, 2)
        variance(0, 0)
        queries(0, 0)
        dve.wait_ge(s_qhi, 1)
        nc.vector.tensor_tensor(q_lo[0][:], q32[:], as_f32(q_hi[0][:]), ALU.subtract).then_inc(s_qlo, 1)
        h, n = over_heads(dve, slot)
        low_probs(n - 1, JB - 1, 0)
        low_probs(n - 2, JB - 2, 1)
        low_probs(n - 1, JB - 1, 1)
        low_first(0)
        gains(h - 1, 1, 1)
        scale_attended(h - 1, n - JB, 0)
        low_first(1)
        normalise_first(2)
        low_first(2)
        normalise_first(3)
        for u in range(3, 2 * FIRST):
            low_first(u)
        scale_attended(h - 1, n - JB, 1)

    return sync, gpsimd, scalar, tensor, vector


def mixture(nc, sem, x1, shared, out):
    rows, D = x1.shape
    tiles = rows // P
    GT = BANK // P
    groups = tiles // GT
    KB = D // P
    E = shared["w2_raw"].shape[2]
    KR = shared["v_hi"].shape[2]
    RB = KR // P
    assert D == 2 * BANK and KR == BANK and RB == 4 and GT == FIRST and KB == 2 * GT
    w1_raw, w1_hi, w1_lo = shared["w1_raw"], shared["w1_hi"], shared["w1_lo"]
    v_raw, v_hi, v_lo = shared["v_raw"], shared["v_hi"], shared["v_lo"]
    u_raw, u_hi, u_lo = shared["u_raw"], shared["u_hi"], shared["u_lo"]
    w2_both = shared["w2_both"]
    w2_raw, b1_col, b2_row = shared["w2_raw"], shared["b1_col"], shared["b2_row"]

    place = SbufMap(nc, shared["end"])
    x_in, normed = shared["first_n"][:2], shared["first_n"][2:]
    nt_hi, nt_lo = shared["nt_hi"], shared["nt_lo"]
    ht_hi = [place.tensor(f"ht_hi{b}", [P, BANK], F32R) for b in range(2)]
    low, after = SbufMap(nc, place.at), SbufMap(nc, place.at)
    hidden = [place.tensor(f"hidden{b}", [P, BANK]) for b in range(2)]
    ht_lo = [low.tensor(f"ht_lo{b}", [P, BANK], F32R) for b in range(2)]
    logits_t = after.tensor("logits_t", [2 * E, BANK])
    gated = [place.tensor(f"gated{b}", [P, KR]) for b in range(2)]
    gt_hi = [place.tensor(f"gt_hi{b}", [P, RB, P], F32R) for b in range(2)]
    gt_lo = [place.tensor(f"gt_lo{b}", [P, RB, P], F32R) for b in range(2)]
    top = SbufMap(nc, shared["top_at"])
    result = [top.tensor(f"result{b}", [P, BANK]) for b in range(4)]
    ident, minus_half = shared["ident"], shared["minus_half"]
    stats = place.tensor("stats2", [P, 12])
    mean_var = [place.tensor(f"mean_var2{k}", [P, 2]) for k in range(GT)]
    var_eps = [place.tensor(f"var_eps{k}", [P, 1]) for k in range(GT)]
    rstd = [place.tensor(f"rstd{k}", [P, 1]) for k in range(GT)]
    logit_part = place.tensor("logit_part", [P, GT, E])
    logits = place.tensor("logits", [P, GT, E])
    centred = place.tensor("centred", [P, GT, E])
    neg_max = place.tensor("neg_max2", [P, GT])
    e_logits = place.tensor("e_logits", [P, GT, E])
    e_sum = place.tensor("e_sum", [P, GT])
    inv_sum = place.tensor("inv_sum2", [P, GT])
    alpha = place.tensor("alpha", [P, GT, E])

    assert place.at <= shared["top_at"]

    turned, work, lt_ps, l_ps, y_ps = (shared[name] for name in ("turned", "work", "lt_ps", "l_ps", "y_ps"))

    s_u_in = sem("s_u_in")
    s_w2, s_whi, s_wlo = sem("s_w2"), sem("s_whi"), sem("s_wlo")
    s_xin = [sem(f"s_xin{b}") for b in range(2)]
    s_stat, s_stats, s_var, s_rstd, s_normed = (sem("s_stat2"), sem("s_stats2"), sem("s_var2"),
                                                sem("s_rstd"), sem("s_normed"))
    s_turn, s_hi, s_lo = shared["s_turn"], shared["s_hi"], shared["s_lo"]
    s_hidden, s_hhi, s_relu, s_hlo = sem("s_hidden"), sem("s_hhi"), sem("s_relu"), sem("s_hlo")
    s_route, s_lt_out, s_l = sem("s_route"), sem("s_lt_out"), sem("s_l")
    s_lpart, s_logits, s_negmax, s_centred, s_exp, s_esum, s_inv, s_alpha = (
        sem("s_lpart"), sem("s_logits"), sem("s_negmax"), sem("s_centred"), sem("s_exp2"), sem("s_esum"),
        sem("s_inv2"), sem("s_alpha"))
    s_v, s_gated = sem("s_v"), sem("s_gated")
    s_y, s_yadd = [sem(f"s_y{b}") for b in range(2)], sem("s_yadd")
    s_res, s_out = ([sem(f"{n}{b}") for b in range(4)] for n in ("s_res", "s_out"))

    def over_groups(eng, slot):
        slot(0, True, False)
        with eng.Fori(1, groups - 1) as g:
            slot(g, False, False)
        slot(groups - 1, False, True)

    LEAD = 2 * GT

    def next_n(k):
        return [("n", k, 0), ("n", k, 1)]

    def units_of(last):
        beside = {"v1": next_n(0), "v2": next_n(1), "v3": [("g", 0, 0)] + next_n(2),
                  "u0": [("g", 1, 0)] + next_n(3), "u1": [("g", 2, 0)], "u2": [("g", 3, 0)]}
        if last:
            beside = {stage: [u for u in units if u[0] == "g"] for stage, units in beside.items()}
        number, numbered = 0, {}
        for stage, units in beside.items():
            numbered[stage] = [(number + i, *u) for i, u in enumerate(units)]
            number += len(units)
        return numbered

    UNITS = 3 * GT
    STATISTICS_AT = (1, 2, 4, 5)

    cols = [slice(e * P, (e + 1) * P) for e in range(KB)]
    chunks = [(w1_raw[:, :, c], w1_hi[:, :, c], w1_lo[:, :, c]) for c in cols]
    chunks += [(v_raw[:, k:k + 2, :], v_hi[:, k:k + 2, :], v_lo[:, k:k + 2, :]) for k in range(0, KB, 2)]
    v_ready = len(chunks)
    chunks += [(u_raw[:, k, :], u_hi[:, k, :], u_lo[:, k, :]) for k in range(RB)]

    def chunks_at(e):
        return range(2 * e + 1, min(2 * e + 3, len(chunks)))

    def sync(sp):
        def load(t, b):
            sp.dma_start(x_in[b][:], x1[bass.ts(t, P), :]).then_inc(s_xin[b], 16)

        def load_residual(g, i):
            b = i % 4
            if not (isinstance(g, int) and g == 0 and i < 4):
                sp.wait_ge(s_out[b], g * 32 + (i // 4) * 16)
            sp.dma_start(result[b][:], x1[bass.ts(g * GT + i // 2, P), i % 2 * BANK:(i % 2 + 1) * BANK]
                         ).then_inc(s_res[b], 16)

        def store(g, i):
            sp.wait_ge(s_yadd, g * (2 * GT) + (i + 1))
            sp.dma_start(out[bass.ts(g * GT + i // 2, P), i % 2 * BANK:(i % 2 + 1) * BANK],
                         result[i % 4][:]).then_inc(s_out[i % 4], 16)

        def slot(g, first, last):
            if not last:
                for k in range(GT):
                    if first and k < 2:
                        sp.wait_ge(s_turn, LEAD)
                    else:
                        sp.wait_ge(s_normed, g * GT + (k - 1))
                    load(g * GT + (GT + k), k % 2)
                    if first and k == 1:
                        sp.wait_ge(shared["s_pv"], tiles * KB)
                        sp.dma_start(u_raw[:], shared["u_dram"]).then_inc(s_u_in, 16)
            for i in range(4):
                load_residual(g, i)
            store(g, 0)
            for i in range(1, 5):
                store(g, i)
                load_residual(g, i + 3)
            for i in range(5, 2 * GT):
                store(g, i)

        for s in shared["s_x1"]:
            sp.wait_ge(s, 16 * tiles)
        over_groups(sp, slot)
        for b in range(4):
            sp.wait_ge(s_out[b], groups * 32)

    def gpsimd(pool):
        def factor(g, k):
            pool.wait_ge(s_var, g * GT + (k + 1))
            nc.gpsimd.tensor_tensor(rstd[k][:], var_eps[k][:], minus_half[:], ALU.pow).then_inc(s_rstd, 1)

        def slot(g, first, last):
            if not last:
                for k in range(GT):
                    factor(g, k)

        over_groups(pool, slot)

    def scalar(act):
        def split_weights(n):
            raw, hi, lo = chunks[n]
            if n == v_ready:
                act.wait_ge(s_u_in, 16)
            nc.scalar.activation(hi, raw, ACT.Copy).then_inc(s_whi, 1)

        def high_hidden(g, e):
            act.wait_ge(s_hidden, g * KB + (e + 1))
            if not (isinstance(g, int) and g == 0 and e < 2):
                act.wait_ge(s_route, g * KB + (e - 1))
            nc.scalar.activation(hidden[e % 2][:], work[e % 2], ACT.Relu,
                                 bias=b1_col[:, e:e + 1]).then_inc(s_relu, 1)
            act.wait_ge(s_relu, g * KB + (e + 1))
            nc.scalar.activation(ht_hi[e % 2][:], hidden[e % 2][:], ACT.Copy).then_inc(s_hhi, 1)

        def high_unit(g, number, what, k, c, used):
            act.wait_ge(s_turn, g * UNITS + (LEAD + number + 1))
            if used is not None:
                act.wait_ge(s_v if what == "n" else s_y[1], used)
            dst = nt_hi[:, 4 * c:4 * c + 4, k * P:(k + 1) * P] if what == "n" else gt_hi[k % 2][:]
            nc.scalar.activation(dst, turned[number % 2], ACT.Copy).then_inc(s_hi, 1)

        def slot(g, first, last):
            for e in range(KB):
                if first:
                    for n in chunks_at(e):
                        split_weights(n)
                high_hidden(g, e)
            act.wait_ge(s_route, g * KB + KB)
            nc.scalar.activation(logits_t[:], lt_ps[0:2 * E, :], ACT.Copy).then_inc(s_lt_out, 1)
            act.wait_ge(s_centred, g + 1)
            nc.scalar.activation(e_logits[:], centred[:], ACT.Exp).then_inc(s_exp, 1)
            for stage, units in units_of(last).items():
                for number, what, k, c in units:
                    if what == "n":
                        used = g * GT + (k + 1)
                    else:
                        used = None if (first and k < 2) else g * GT + (k - 1)
                    high_unit(g, number, what, k, c, used)

        act.wait_ge(shared["s_pre"], 16 * len(shared["loads"]))
        nc.scalar.activation(w2_both[:, :, 0:E], w2_raw[:], ACT.Copy).then_inc(s_w2, 1)
        act.wait_ge(shared["s_added"], 2 * tiles)
        over_groups(act, slot)

    def tensor(pe):
        mm = nc.tensor.matmul

        def hidden_products(g, e):
            def product(k, i):
                if k == 0 and i == 0:
                    if e == 0:
                        pe.wait_ge(s_lo, g * UNITS + LEAD)
                    if isinstance(g, int) and g == 0 and e == 0:
                        pe.wait_ge(shared["s_w_first"], 2)
                    elif isinstance(g, int) and g == 0:
                        pe.wait_ge(s_wlo, e)
                    if e >= 2:
                        pe.wait_ge(s_relu, g * KB + (e - 1))
                    elif not (isinstance(g, int) and g == 0):
                        pe.wait_ge(s_gated, g * GT + (e - 1))
                w, n = ((w1_hi, nt_hi), (w1_lo, nt_hi), (w1_hi, nt_lo))[i]
                ins = mm(work[e % 2], w[:, k, cols[e]], n[:, k, :], start=(k == 0 and i == 0),
                         stop=(k == KB - 1 and i == 2))
                if k == KB - 1 and i == 2:
                    ins.then_inc(s_hidden, 1)
            return [lambda k=k, i=i: product(k, i) for k in range(KB) for i in range(3)]

        def router_products(g, e):
            def product(i):
                if i == 0:
                    pe.wait_ge(s_hlo, g * KB + (e + 1))
                    if e == 0 and isinstance(g, int) and g == 0:
                        pe.wait_ge(s_w2, 2)
                    elif e == 0:
                        pe.wait_ge(s_lt_out, g)
                    mm(lt_ps[0:2 * E, :], w2_both[:, e, :], ht_hi[e % 2][:], start=(e == 0),
                       stop=(e == KB - 1), skip_group_check=True)
                else:
                    mm(lt_ps[0:E, :], w2_both[:, e, 0:E], ht_lo[e % 2][:], start=False,
                       stop=(e == KB - 1), skip_group_check=True).then_inc(s_route, 1)
            return [lambda i=i: product(i) for i in range(2)]

        def turn_logits(g):
            def turn(k):
                ins = pe.transpose(l_ps[:, k, 0:2 * E], logits_t[:, k * P:(k + 1) * P],
                                   ident[0:2 * E, 0:2 * E])
                if k == GT - 1:
                    ins.then_inc(s_l, 1)
            return [lambda k=k: turn(k) for k in range(GT)]

        def value_products(g, k):
            def product(d, i):
                if d == 0 and i == 0:
                    if isinstance(g, int) and g == 0 and k == 0:
                        pe.wait_ge(s_wlo, v_ready - 1)
                    if k < 2:
                        pe.wait_ge(s_relu, g * KB + (KB + k - 1))
                    else:
                        pe.wait_ge(s_gated, g * GT + (k - 1))
                n, w = ((nt_hi, v_hi), (nt_hi, v_lo), (nt_lo, v_hi))[i]
                ins = mm(work[k % 2], n[:, d, k * P:(k + 1) * P], w[:, d, :], start=(d == 0 and i == 0),
                         stop=(d == KB - 1 and i == 2))
                if d == KB - 1 and i == 2:
                    ins.then_inc(s_v, 1)
            return [lambda d=d, i=i: product(d, i) for d in range(KB) for i in range(3)]

        def expert_products(g, k, unit):
            def product(c, r, i):
                if r == 0 and i == 0:
                    if c == 0:
                        pe.wait_ge(s_lo, g * UNITS + (LEAD + unit + 1))
                        if isinstance(g, int) and g == 0 and k == 0:
                            pe.wait_ge(s_wlo, len(chunks) - 1)
                    if not (isinstance(g, int) and g == 0 and k == 0):
                        pe.wait_ge(s_yadd, g * (2 * GT) + (2 * k + c - 1))
                w, u = ((gt_hi, u_hi), (gt_hi, u_lo), (gt_lo, u_hi))[i]
                ins = mm(y_ps[c], w[k % 2][:, r, :], u[:, r, c * BANK:(c + 1) * BANK],
                         start=(r == 0 and i == 0), stop=(r == RB - 1 and i == 2))
                if r == RB - 1 and i == 2:
                    ins.then_inc(s_y[c], 1)
            return [lambda c=c, r=r, i=i: product(c, r, i) for c in range(2) for r in range(RB)
                    for i in range(3)]

        def turn_unit(g, number, what, k, c):
            def turn(i):
                if i == 0:
                    if what == "n":
                        pe.wait_ge(s_normed, g * GT + (k + 1))
                    else:
                        pe.wait_ge(s_gated, g * GT + (k + 1))
                    if not (isinstance(g, int) and g * UNITS + LEAD + number < 2):
                        pe.wait_ge(s_lo, g * UNITS + (LEAD + number - 1))
                src = normed[k % 2][:, (4 * c + i) * P:(4 * c + i + 1) * P] if what == "n" else \
                    gated[k % 2][:, i * P:(i + 1) * P]
                ins = pe.transpose(turned[number % 2][:, i, :], src, ident[:])
                if i == 3:
                    ins.then_inc(s_turn, 1)
            return [lambda i=i: turn(i) for i in range(4)]

        def issue_all(functions):
            for issue in functions:
                issue()

        def slot(g, first, last):
            beside = units_of(last)
            for e in range(KB):
                big = hidden_products(g, e)
                issue_all(big[:12] + (router_products(g, e - 1) if e else []) + big[12:])

            def turns_at(stage):
                return [turn for unit in beside.get(stage, []) for turn in turn_unit(g, *unit)]

            big = value_products(g, 0)
            issue_all(big[:12] + router_products(g, KB - 1) + big[12:20])
            pe.wait_ge(s_lt_out, g + 1)
            if not (isinstance(g, int) and g == 0):
                pe.wait_ge(s_logits, g)
            issue_all(interleave(big[20:], turn_logits(g), 1, 2))
            for k in range(1, GT):
                issue_all(interleave(value_products(g, k), turns_at(f"v{k}"), 4, 1))
            gated_unit = {k: number for units in beside.values() for number, what, k, c in units
                          if what == "g"}
            for k in range(GT):
                issue_all(interleave(expert_products(g, k, gated_unit[k]), turns_at(f"u{k}"), 2, 1))

        over_groups(pe, slot)

    def vector(dve):
        def statistics(g, k):
            b = k % 2
            dve.wait_ge(s_xin[b], g * 32 + (k // 2 * 16 + 16))
            for c in range(2):
                nc.vector.bn_stats(stats[:, 6 * c:6 * c + 6],
                                   x_in[b][:, c * BANK:(c + 1) * BANK]).then_inc(s_stat, 1)

        def variance(g, k):
            nc.vector.bn_aggr(mean_var[k][:], stats[:]).then_inc(s_stats, 1)
            dve.wait_ge(s_stats, g * GT + (k + 1))
            nc.vector.tensor_scalar(var_eps[k][:], mean_var[k][:, 1:2], EPS, None, ALU.add).then_inc(s_var, 1)

        def normalise(g, k, turned_units):
            dve.wait_ge(s_rstd, g * GT + (k + 1))
            if turned_units is not None:
                dve.wait_ge(s_turn, turned_units)
            nc.vector.tensor_scalar(normed[k % 2][:], x_in[k % 2][:], mean_var[k][:, 0:1], rstd[k][:],
                                    ALU.subtract, ALU.mult).then_inc(s_normed, 1)

        def low_hidden(g, e):
            dve.wait_ge(s_hhi, g * KB + (e + 1))
            nc.vector.tensor_tensor(ht_lo[e % 2][:], hidden[e % 2][:], as_f32(ht_hi[e % 2][:]),
                                    ALU.subtract).then_inc(s_hlo, 1)

        def low_unit(g, number, what, k, c):
            dve.wait_ge(s_hi, g * UNITS + (LEAD + number + 1))
            at = (slice(None), slice(4 * c, 4 * c + 4), slice(k * P, (k + 1) * P))
            hi, lo = (nt_hi[at], nt_lo[at]) if what == "n" else (gt_hi[k % 2][:], gt_lo[k % 2][:])
            nc.vector.tensor_tensor(lo, turned[number % 2], as_f32(hi), ALU.subtract).then_inc(s_lo, 1)

        def split_weights(n):
            raw, hi, lo = chunks[n]
            dve.wait_ge(s_whi, n)
            nc.vector.tensor_tensor(lo, raw, as_f32(hi), ALU.subtract).then_inc(s_wlo, 1)

        def softmax(g):
            dve.wait_ge(s_l, g + 1)
            nc.vector.tensor_tensor(logit_part[:], l_ps[:, :, 0:E], b2_row[:].unsqueeze(1).to_broadcast([P, GT, E]),
                                    ALU.add).then_inc(s_lpart, 1)
            dve.wait_ge(s_lpart, g + 1)
            nc.vector.tensor_tensor(logits[:], l_ps[:, :, E:2 * E], logit_part[:], ALU.add).then_inc(s_logits, 1)
            dve.wait_ge(s_logits, g + 1)
            nc.vector.tensor_reduce(neg_max[:], logits[:], AX_X, ALU.max, negate=True).then_inc(s_negmax, 1)
            dve.wait_ge(s_negmax, g + 1)
            nc.vector.tensor_tensor(centred[:], logits[:], neg_max[:].unsqueeze(2).to_broadcast([P, GT, E]),
                                    ALU.add).then_inc(s_centred, 1)
            dve.wait_ge(s_exp, g + 1)
            nc.vector.tensor_reduce(e_sum[:], e_logits[:], AX_X, ALU.add).then_inc(s_esum, 1)
            dve.wait_ge(s_esum, g + 1)
            nc.vector.reciprocal(inv_sum[:], e_sum[:]).then_inc(s_inv, 1)
            dve.wait_ge(s_inv, g + 1)
            nc.vector.tensor_tensor(alpha[:], e_logits[:], inv_sum[:].unsqueeze(2).to_broadcast([P, GT, E]),
                                    ALU.mult).then_inc(s_alpha, 1)

        def gate(g, k, turned_units):
            dve.wait_ge(s_v, g * GT + (k + 1))
            if k == 0:
                dve.wait_ge(s_alpha, g + 1)
            if turned_units is not None:
                dve.wait_ge(s_turn, turned_units)
            nc.vector.tensor_tensor(gated[k % 2][:].rearrange("p (e r) -> p e r", e=E),
                                    work[k % 2].rearrange("p (e r) -> p e r", e=E),
                                    alpha[:, k, :].unsqueeze(2).to_broadcast([P, E, KR // E]),
                                    ALU.mult).then_inc(s_gated, 1)

        def add_residual(g, i):
            dve.wait_ge(s_y[i % 2], g * GT + (i // 2 + 1))
            dve.wait_ge(s_res[i % 4], g * 32 + (i // 4 * 16 + 16))
            nc.vector.tensor_tensor(result[i % 4][:], y_ps[i % 2], result[i % 4][:],
                                    ALU.add).then_inc(s_yadd, 1)

        def slot(g, first, last):
            beside = units_of(last)

            def turned_after(what, k):
                number = max(n for units in beside.values() for n, w, tile, c in units if (w, tile) == (what, k))
                return g * UNITS + (LEAD + number + 1)

            def low_units(stage):
                for unit in beside.get(stage, []):
                    low_unit(g, *unit)

            for e in range(KB):
                if first:
                    for n in chunks_at(e):
                        split_weights(n)
                if e in STATISTICS_AT and not last:
                    k = STATISTICS_AT.index(e)
                    statistics(g, k)
                    dve.wait_ge(s_stat, g * (2 * GT) + (2 * k + 2))
                low_hidden(g, e)
                if e in STATISTICS_AT and not last:
                    variance(g, k)
                    if k < 2:
                        normalise(g, k, g * UNITS + LEAD)
            softmax(g)
            gate(g, 0, None if first else g * UNITS + LEAD)
            low_units("v1")
            gate(g, 1, None if first else g * UNITS + LEAD)
            low_units("v2")
            if not last:
                normalise(g, 2, turned_after("n", 0))
            gate(g, 2, turned_after("g", 0))
            low_units("v3")
            if not last:
                normalise(g, 3, turned_after("n", 1))
            gate(g, 3, turned_after("g", 1))
            for k in range(GT):
                low_units(f"u{k}")
                add_residual(g, 2 * k)
                add_residual(g, 2 * k + 1)

        dve.wait_ge(s_w2, 1)
        nc.vector.tensor_tensor(w2_both[:, :, E:2 * E], w2_raw[:], as_f32(w2_both[:, :, 0:E]),
                                ALU.subtract).then_inc(s_w2, 1)
        over_groups(dve, slot)

    return sync, gpsimd, scalar, tensor, vector


def cross_attention_and_mixture(nc, x, ctx, ctx_t, gamma, u_t, v_t, w1, b1_t, w2, b2, out):
    D, KR = v_t.shape
    E = w2.shape[1]
    KB, RB = D // P, KR // P
    x1 = nc.dram_tensor("x1", tuple(x.shape), F32, kind="Internal").ap()
    scratch = nc.dram_tensor("gains", (2 * x.shape[0] // P, BANK), F32, kind="Internal").ap()

    place = SbufMap(nc, (nc.sbuf_base + 31) // 32 * 32)
    shared = {
        "w2_raw": place.tensor("w2_raw", [P, KB, E]),
        "w2_both": place.tensor("w2_both", [P, KB, 2 * E], F32R),
        "b1_col": place.tensor("b1_col", [P, KB]),
        "b2_row": place.tensor("b2_row", [P, E]),
        "ident": place.tensor("ident", [P, P]),
        "minus_half": place.tensor("minus_half", [P, 1]),
        "zero_col": place.tensor("zero_col", [P, 1]),
    }

    def place_raw(name, blocks, width):
        low = SbufMap(nc, place.at)
        shared[name + "_raw"] = place.tensor(name + "_raw", [P, blocks, width])
        shared[name + "_lo"] = low.tensor(name + "_lo", [P, blocks, width], F32R)

    place_raw("w1", KB, D)
    place_raw("v", KB, KR)
    shared["loaded_end"] = place.at
    shared["w1_hi"] = place.tensor("w1_hi", [P, KB, D], F32R)
    place_raw("u", RB, D)
    shared["v_hi"] = place.tensor("v_hi", [P, KB, KR], F32R)
    shared["first_at"] = place.at
    shared["first_n"] = [place.tensor(f"first_n{k}", [P, D]) for k in range(FIRST)]
    shared["nt_at"] = place.at
    shared["nt_hi"] = place.tensor("nt_hi", [P, KB, BANK], F32R)
    shared["nt_lo"] = place.tensor("nt_lo", [P, KB, BANK], F32R)
    shared["u_hi"] = place.tensor("u_hi", [P, RB, D], F32R)
    shared["end"] = place.at
    shared["top_at"] = nc.sbuf_usable_end // 32 * 32 - 4 * BANK * 4

    w1_rows, v_rows = (a.rearrange("(k p) n -> p k n", p=P) for a in (w1, v_t))
    shared["loads"] = [(shared["w2_raw"][:], w2.rearrange("(k p) e -> p k e", p=P)),
                       (shared["b1_col"][:], b1_t),
                       (shared["b2_row"][:], b2.partition_broadcast(P))]
    shared["loads"] += [(shared["w1_raw"][:, k, :], w1_rows[:, k, :]) for k in range(KB)]
    shared["loads"] += [(shared["v_raw"][:, k:k + 2, :], v_rows[:, k:k + 2, :]) for k in range(0, KB, 2)]
    cols = slice(0, P)
    shared["first_weights"] = tuple(shared[name][:, :, cols] for name in ("w1_raw", "w1_hi", "w1_lo"))
    shared["u_dram"] = u_t.rearrange("(k p) d -> p k d", p=P)
    with ExitStack() as stack:
        def sem(name):
            return stack.enter_context(nc.semaphore(name))

        def psum(name, shape):
            return stack.enter_context(nc.psum_tensor(name, shape, F32))

        for name in ("s_pre", "s_const", "s_pv", "s_added", "s_turn", "s_hi", "s_lo", "s_w_first"):
            shared[name] = sem(name)
        shared["s_x1"] = [sem(f"s_x1{b}") for b in range(2)]
        scores = shared["scores"] = [psum(f"scores{b}", [P, 2 * BANK]) for b in range(2)]
        turned0 = shared["turned0"] = psum("turned0", [P, 4, P])
        turned1 = shared["turned1"] = [psum(f"turned1{b}", [P, 4, P]) for b in range(2)]
        attended = shared["attended"] = psum("attended", [P, BANK])
        halves = [slice(c * BANK, (c + 1) * BANK) for c in range(2)]
        shared["turned"] = [scores[0][:, half].rearrange("p (i n) -> p i n", n=P) for half in halves]
        shared["work"] = [scores[1][:, half] for half in halves]
        shared["lt_ps"] = turned0[:].rearrange("p i n -> p (i n)")
        shared["l_ps"] = turned1[0]
        shared["y_ps"] = [turned1[1][:].rearrange("p i n -> p (i n)"), attended[:]]

        parts = (attention(nc, sem, x, ctx, ctx_t, gamma, x1, scratch, shared), mixture(nc, sem, x1, shared, out))
        block = stack.enter_context(nc.Block())

        @block.sync
        def _(sp):
            for sync, *_ in parts:
                sync(sp)

        @block.gpsimd
        def _(pool):
            for _, gpsimd, *_ in parts:
                gpsimd(pool)

        @block.scalar
        def _(act):
            for _, _, scalar, *_ in parts:
                scalar(act)

        @block.tensor
        def _(pe):
            for *_, tensor, _ in parts:
                tensor(pe)

        @block.vector
        def _(dve):
            for *_, vector in parts:
                vector(dve)


def kernel(**inputs):
    import numpy as np
    import concourse.bacc as bacc
    from concourse.bass_utils import run_bass_kernel_spmd

    x = np.asarray(inputs["x"])
    ctx = np.asarray(inputs["ctx_2048"])
    B, S, D = x.shape
    heads = B * S // P
    U, V = np.asarray(inputs["L0_ffn_U"]), np.asarray(inputs["L0_ffn_V"])
    experts, _, rank = U.shape
    ctx_t = ctx.reshape(heads, P, D // P, P).transpose(0, 3, 2, 1)
    arrays = {
        "x": x.reshape(B * S, D),
        "ctx": ctx.reshape(B * S, D),
        "ctx_t": ctx_t.reshape(B * S, D),
        "gamma": np.asarray(inputs["L0_xattn_gamma"]).reshape(1, 1),
        "u_t": U.transpose(0, 2, 1).reshape(experts * rank, D),
        "v_t": V.reshape(experts * rank, D).transpose(1, 0),
        "w1": np.asarray(inputs["L0_ffn_W1"]),
        "b1_t": np.asarray(inputs["L0_ffn_b1"]).reshape(D // P, P).transpose(1, 0),
        "w2": np.asarray(inputs["L0_ffn_W2"]),
        "b2": np.asarray(inputs["L0_ffn_b2"]),
    }
    arrays = {"in_" + name: np.ascontiguousarray(a) for name, a in arrays.items()}
    nc = bacc.Bacc("TRN2", target_bir_lowering=False, num_devices=1)
    args = [nc.dram_tensor(name, a.shape, mybir.dt.from_np(a.dtype), kind="ExternalInput").ap()
            for name, a in arrays.items()]
    args.append(nc.dram_tensor("out", (B * S, D), F32, kind="ExternalOutput").ap())
    cross_attention_and_mixture(nc, *args)
    result = run_bass_kernel_spmd(nc, [arrays], core_ids=[0])
    return result.results[0]["out"].reshape(B, S, D)
```
